# Optimizing a Trainium2 kernel written in Bass

```python
import numpy as np
import jax
import jax.numpy as jnp

def _softmax(x, axis=-1):
    return jax.nn.softmax(x, axis=axis)

def _gelu(x):
    return jax.nn.gelu(x, approximate=True)

def _silu(x):
    return jax.nn.silu(x)

def _sigmoid(x):
    return jax.nn.sigmoid(x)

def _layernorm(x, axis=-1, eps=1e-05):
    m = jnp.mean(x, axis=axis, keepdims=True)
    v = jnp.var(x, axis=axis, keepdims=True)
    return (x - m) / jnp.sqrt(v + eps)

def _scatter_add(tgt, idx, src, axis=0):
    return tgt.at[idx].add(src)

def _segment_sum(src, seg, n):
    return jax.ops.segment_sum(src, seg, n)
kernel_name = 'mk_lm_tower_d1_tok_ids512_r4_4382d6'

def setup_inputs(seed: int=0):
    np.random.seed(seed)
    _w = jnp.asarray

    def _rec_inputs():
        import jax
        import jax.numpy as jnp
        _rk = jax.random.key(seed)
        x = jax.random.randint(jax.random.fold_in(_rk, 1), (2, 1024), 0, 125, jnp.int32)
        return x
    x = _rec_inputs()

    def _L0_tok_setup():
        import jax, jax.numpy as jnp
        import numpy as np
        QMAX = 127.0
        CTX = 2

        def fake_quant(w):
            scale = jnp.max(jnp.abs(w)) / QMAX
            wq = jnp.round(w / scale) * scale
            return w + jax.lax.stop_gradient(wq - w)
        key = jax.random.key(seed)
        k1, k2, k3 = jax.random.split(key, 3)
        y = jax.random.randint(k1, (64, 512), 0, 125, dtype=jnp.int64)
        emb_weight = jax.random.normal(k2, (125, 128), dtype=jnp.float32)
        conv_weight = jax.random.normal(k3, (128, 1, 2), dtype=jnp.float32)
        return {'y': y, 'emb_weight': emb_weight, 'conv_weight': conv_weight}
    _L0_tok_all = _L0_tok_setup()
    _L0_tok_in = {k: v for k, v in _L0_tok_all.items() if k in ('emb_weight', 'conv_weight')}
    del _L0_tok_all

    def _L0_attn_setup():
        import jax, jax.numpy as jnp
        import numpy as np
        HEADS = 8
        DIM_HEAD = 64
        NEG_MAX = -jnp.finfo(jnp.float32).max

        def _sn_weight(W, u, sigma):
            v = jax.lax.stop_gradient(W @ u)
            v = v / jnp.linalg.norm(v)
            u2 = jax.lax.stop_gradient(W.T @ v)
            u2 = u2 / jnp.linalg.norm(u2)
            v = jax.lax.stop_gradient(v)
            u2 = jax.lax.stop_gradient(u2)
            sig = jnp.einsum('c,cd,d->', v, W, u2)
            return W / sig * sigma
        key = jax.random.key(seed)
        ks = jax.random.split(key, 5)
        dim, inner = (128, HEADS * DIM_HEAD)
        x = jax.random.normal(ks[0], (4, 512, dim), dtype=jnp.float32)
        w_qkv = 0.02 * jax.random.normal(ks[1], (3 * inner, dim), dtype=jnp.float32)
        u_qkv = jax.random.normal(ks[2], (dim,), dtype=jnp.float32)
        u_qkv = u_qkv / jnp.linalg.norm(u_qkv)
        w_out = 0.02 * jax.random.normal(ks[3], (dim, inner), dtype=jnp.float32)
        b_out = jnp.zeros((dim,), dtype=jnp.float32)
        u_out = jax.random.normal(ks[4], (inner,), dtype=jnp.float32)
        u_out = u_out / jnp.linalg.norm(u_out)
        sigma_qkv = jnp.array(1.0, dtype=jnp.float32)
        sigma_out = jnp.array(1.0, dtype=jnp.float32)
        temperature = jnp.log(jnp.array(DIM_HEAD ** (-0.5), dtype=jnp.float32))
        return {'x': x, 'w_qkv': w_qkv, 'u_qkv': u_qkv, 'sigma_qkv': sigma_qkv, 'w_out': w_out, 'b_out': b_out, 'u_out': u_out, 'sigma_out': sigma_out, 'temperature': temperature}
    _L0_attn_all = _L0_attn_setup()
    _L0_attn_in = {k: v for k, v in _L0_attn_all.items() if k in ('w_qkv', 'u_qkv', 'sigma_qkv', 'w_out', 'b_out', 'u_out', 'sigma_out', 'temperature')}
    del _L0_attn_all

    def _L0_ffn_setup():
        import jax, jax.numpy as jnp
        import numpy as np
        NEXPERTS = 16
        key = jax.random.key(seed)
        k1, k2, k3, k4 = jax.random.split(key, 4)
        B, S, D = (4, 512, 128)
        E, Sets, F = (16, 4, 32)
        scale = 0.02
        return {'x': jax.random.normal(k1, (B, S, D), dtype=jnp.float32), 'controller': jax.random.normal(k2, (D, E, Sets), dtype=jnp.float32) * scale, 'f1': jax.random.normal(k3, (D, E, Sets, F), dtype=jnp.float32) * scale, 'f2': jax.random.normal(k4, (E, Sets, F, D), dtype=jnp.float32) * scale}
    _L0_ffn_all = _L0_ffn_setup()
    _L0_ffn_in = {k: v for k, v in _L0_ffn_all.items() if k in ('controller', 'f1', 'f2')}
    del _L0_ffn_all
    return {'x': x, 'L0_tok_emb_weight': _L0_tok_in['emb_weight'], 'L0_tok_conv_weight': _L0_tok_in['conv_weight'], 'L0_attn_w_qkv': _L0_attn_in['w_qkv'], 'L0_attn_u_qkv': _L0_attn_in['u_qkv'], 'L0_attn_sigma_qkv': _L0_attn_in['sigma_qkv'], 'L0_attn_w_out': _L0_attn_in['w_out'], 'L0_attn_b_out': _L0_attn_in['b_out'], 'L0_attn_u_out': _L0_attn_in['u_out'], 'L0_attn_sigma_out': _L0_attn_in['sigma_out'], 'L0_attn_temperature': _L0_attn_in['temperature'], 'L0_ffn_controller': _L0_ffn_in['controller'], 'L0_ffn_f1': _L0_ffn_in['f1'], 'L0_ffn_f2': _L0_ffn_in['f2']}

def reference(x, L0_tok_emb_weight, L0_tok_conv_weight, L0_attn_w_qkv, L0_attn_u_qkv, L0_attn_sigma_qkv, L0_attn_w_out, L0_attn_b_out, L0_attn_u_out, L0_attn_sigma_out, L0_attn_temperature, L0_ffn_controller, L0_ffn_f1, L0_ffn_f2):
    import jax
    import jax.numpy as jnp

    def _L0_tok_ref(y, emb_weight, conv_weight):
        import jax, jax.numpy as jnp
        import numpy as np
        QMAX = 127.0
        CTX = 2

        def fake_quant(w):
            scale = jnp.max(jnp.abs(w)) / QMAX
            wq = jnp.round(w / scale) * scale
            return w + jax.lax.stop_gradient(wq - w)
        w_emb = fake_quant(emb_weight)
        e = w_emb[jnp.clip(y, 0)]
        e = e * (y >= 0)[..., None].astype(e.dtype)
        x = jnp.pad(e, ((0, 0), (CTX - 1, 0), (0, 0)))
        D = conv_weight.shape[0]
        w = fake_quant(conv_weight).transpose(2, 1, 0)
        out = jax.lax.conv_general_dilated(x, w, window_strides=(1,), padding='VALID', feature_group_count=D, dimension_numbers=('NWC', 'WIO', 'NWC'))
        return jax.nn.relu(out)

    def _L0_attn_ref(x, w_qkv, u_qkv, sigma_qkv, w_out, b_out, u_out, sigma_out, temperature):
        import jax, jax.numpy as jnp
        import numpy as np
        HEADS = 8
        DIM_HEAD = 64
        NEG_MAX = -jnp.finfo(jnp.float32).max

        def _sn_weight(W, u, sigma):
            v = jax.lax.stop_gradient(W @ u)
            v = v / jnp.linalg.norm(v)
            u2 = jax.lax.stop_gradient(W.T @ v)
            u2 = u2 / jnp.linalg.norm(u2)
            v = jax.lax.stop_gradient(v)
            u2 = jax.lax.stop_gradient(u2)
            sig = jnp.einsum('c,cd,d->', v, W, u2)
            return W / sig * sigma
        b, n, _ = x.shape
        Wq = _sn_weight(w_qkv, u_qkv, sigma_qkv)
        qkv = x @ Wq.T
        q, k, v = jnp.split(qkv, 3, axis=-1)

        def heads(t):
            return t.reshape(b, n, HEADS, DIM_HEAD).transpose(0, 2, 1, 3)
        q, k, v = (heads(q), heads(k), heads(v))
        dots = jnp.einsum('bhid,bhjd->bhij', q, k) * jnp.exp(temperature)
        eye = jnp.eye(n, dtype=bool)
        dots = jnp.where(eye, NEG_MAX, dots)
        attn = jax.nn.softmax(dots, axis=-1)
        out = jnp.einsum('bhij,bhjd->bhid', attn, v)
        out = out.transpose(0, 2, 1, 3).reshape(b, n, HEADS * DIM_HEAD)
        Wo = _sn_weight(w_out, u_out, sigma_out)
        return out @ Wo.T + b_out

    def _L0_ffn_ref(x, controller, f1, f2):
        import jax, jax.numpy as jnp
        import numpy as np
        NEXPERTS = 16
        B, S, D = x.shape
        t = NEXPERTS
        grouped = x.reshape(B, S // t, t, D)
        cont_logits = jnp.einsum('bgtd,des->bgtes', grouped, controller)
        tie = jnp.linspace(0.0, 1e-06, t, dtype=x.dtype).reshape(t, 1, 1)
        cont_logits = cont_logits + tie
        cont_perm = (cont_logits == jnp.max(cont_logits, axis=-3, keepdims=True)).astype(x.dtype)
        intermediate = jnp.einsum('bgtd,desf->bgtesf', grouped, f1)
        inner = jnp.einsum('bgtesf,bgtes->bgesf', intermediate, cont_perm)
        inner = jax.nn.relu(inner)
        inter2 = jnp.einsum('bgesf,esfd->bgesd', inner, f2)
        result = jnp.einsum('bgesd,bgtes->bgtd', inter2, cont_perm)
        return result.reshape(B, S, D)
    h = _L0_tok_ref(x, L0_tok_emb_weight, L0_tok_conv_weight)
    h = h + _L0_attn_ref(_layernorm(h, axis=-1), L0_attn_w_qkv, L0_attn_u_qkv, L0_attn_sigma_qkv, L0_attn_w_out, L0_attn_b_out, L0_attn_u_out, L0_attn_sigma_out, L0_attn_temperature)
    h = h + _L0_ffn_ref(_layernorm(h, axis=-1), L0_ffn_controller, L0_ffn_f1, L0_ffn_f2)
    return h

_drawn_inputs = setup_inputs


def setup_inputs(seed=0):
    import zlib

    import numpy as np

    out = dict(_drawn_inputs(seed))
    spreads = {'L0_attn_b_out': (0.0, 0.1)}
    factors = {}
    for name, (base, spread) in spreads.items():
        noise = np.random.default_rng([zlib.crc32(name.encode()), seed]).standard_normal(out[name].shape)
        drawn = base * np.exp(spread * noise) if base else spread * noise
        out[name] = jnp.asarray(drawn.astype(out[name].dtype))
    for name, factor in factors.items():
        out[name] = (out[name] * factor).astype(out[name].dtype)
    return out
```

```python
import numpy as np
from contextlib import ExitStack

import concourse.bass as bass
from concourse import mybir

F32 = mybir.dt.float32
F32R = mybir.dt.float32r
BF16 = mybir.dt.bfloat16
I32 = mybir.dt.int32
ALU = mybir.AluOpType
ACT = mybir.ActivationFunctionType
AXX = mybir.AxisListType.X
MAX_OVER_PARTITIONS = bass.bass_isa.ReduceOp.max

P = 128
B, SEQ, D = 2, 1024, 128
VOCAB = 125
H, DH = 8, 64
NT = SEQ // P
TILES = B * NT
SPH = NT
SPB = H * SPH
CPH = NT // 2
CPB = H * CPH
CW = 2 * P
HALF = SEQ // 2
GROUP = 16
ES = 64
F = 32
PAIRS = B * SEQ // (2 * GROUP)
GROUPS = 2 * PAIRS
PPT = PAIRS // TILES
NK = ES * F // P
QMAX = 127.0
ROUND = 12582912.0
NEG = -3.0e38
EPS = 1e-5
TIE = 1e-6 / (GROUP - 1)
T_LAG, PV_LAG = 3, 5


def layer_kernel(nc, tok, emb, conv, w_heads, wv, wqkv_t, wqkv_rows, u_qkv, wo_dup, wo_rows, u_out,
                 sigma_qkv, sigma_out, temperature, b_out, controller, f1, f2, out):
    with ExitStack() as ctx:
        def sb(name, shape, dt=F32):
            return ctx.enter_context(nc.sbuf_tensor(name, shape, dt))

        def sem(name):
            return ctx.enter_context(nc.semaphore(name))

        ps = ctx.enter_context(nc.psum_tensor("ps", [P, 8, 512], F32))
        SCORES, TRANS, PV_BANK, WORK = 0, 4, 6, 7

        ident = sb("ident", [P, P])
        ident_b = sb("ident_b", [P, P], BF16)
        neg_diag = sb("neg_diag", [P, P], BF16)
        ones = sb("ones", [P, P])
        quad = sb("quad", [P, 4])
        vocab_id = sb("vocab_id", [P, 1])
        tie = sb("tie", [P, GROUP])
        powers = sb("powers", [P, 3 * NT])
        emb_sb = sb("emb_sb", [P, D])
        conv_sb = sb("conv_sb", [P, 2, D])
        quant = sb("quant", [P, 3 * D])
        table = sb("table", [P, 2, D])
        qs = sb("qs", [P, 8])
        wv_sb = sb("wv_sb", [P, H * DH])
        wo_sb = sb("wo_sb", [P, H, D])
        u_sb = sb("u_sb", [P, 1])
        uo_sb = sb("uo_sb", [DH, H])
        sig = sb("sig", [P, 3])
        norm_sb = sb("norm_sb", [P, 32])
        w_slot = sb("w_slot", [P, 2, 2 * P])
        b_sb = sb("b_sb", [P, D])
        h_sb = sb("h_sb", [P, TILES, D])
        x2 = sb("x2", [P, TILES, D])
        x2t = sb("x2t", [P, B * SEQ])
        xt = sb("xt", [P, SEQ])
        stats = sb("stats", [P, NT, 6])
        mv = sb("mv", [P, NT, 2])
        rstd = sb("rstd", [P, NT])
        q_st = sb("q_st", [P, 2, SEQ], F32R)
        k_hi = sb("k_hi", [P, 2, SEQ], F32R)
        k_lo = sb("k_lo", [P, 2, SEQ], F32R)
        v_all = sb("v_all", [P, NT, H, P], F32R)
        v_slot = sb("v_slot", [P, 2, NT, P], F32R)
        probs = sb("probs", [P, 4, SEQ])
        neg_max = sb("neg_max", [P, 4])
        row_sum = sb("row_sum", [P, 4])
        inv_sum = sb("inv_sum", [P, 4])
        pt_hi = sb("pt_hi", [P, 2, NT, CW], F32R)
        pt_lo = sb("pt_lo", [P, 2, NT, CW], F32R)
        o_t = sb("o_t", [P, H, SEQ])
        ctrl_sb = sb("ctrl_sb", [P, ES])
        f1_sb = sb("f1_sb", [P, ES * F])
        f2_sb = sb("f2_sb", [P, NK, D])
        group_max = sb("group_max", [P, PAIRS])

        probs_flat = probs[:, :, :].rearrange("p a b -> p (a b)")
        one_hot = probs_flat[0:VOCAB, 0:SEQ + 1]
        tok_sb = probs_flat[0:VOCAB, 2 * SEQ:3 * SEQ].bitcast(I32)
        perm = x2t[:, :].rearrange("p (j t) -> p j t", t=2 * GROUP)
        x_hat2 = probs_flat[:, 3 * SEQ:4 * SEQ].rearrange("p (t d) -> p t d", d=D)
        logits = probs_flat[:, 0:SEQ]
        hidden = probs_flat[:, SEQ:2 * SEQ].rearrange("p (r n) -> p r n", r=2)
        result = probs_flat[:, 2 * SEQ:4 * SEQ].rearrange("p (t d) -> p t d", d=D)
        o_flat = o_t[:, :, :].rearrange("p h n -> p (h n)")
        x_hat = o_flat[:, 0:SEQ].rearrange("p (t d) -> p t d", d=D)
        wt_sb = o_flat[:, 1024:1024 + 12 * P]
        wr_sb = o_flat[:, 3072:3072 + 12 * P].rearrange("p (t d) -> p t d", d=D)
        wor_sb = o_flat[:, 5120:5120 + H * DH]
        inter_p = o_flat.rearrange("p (j d) -> p j d", d=D)
        v_flat = v_all[:, :, :, :].rearrange("p t h c -> p (t h c)").bitcast(F32)
        taken = v_flat.rearrange("p (e g) -> p e g", g=GROUPS)
        inter_t = v_flat.rearrange("p (j r) -> p j r", r=P)
        pt_hi_flat = pt_hi[:, :, :, :].rearrange("p a t c -> p (a t c)")
        pt_lo_flat = pt_lo[:, :, :, :].rearrange("p a t c -> p (a t c)")
        spread = pt_hi_flat[:, 0:1024].rearrange("p (r j c) -> p r j c", r=2, c=P)
        x2_hi = pt_lo_flat[:, 0:2048].rearrange("p (t d) -> p t d", d=D)
        x2_lo = pt_lo_flat[:, 2048:4096].rearrange("p (t d) -> p t d", d=D)

        wait_passed = sem("wait_passed")
        batch_free = sem("batch_free")
        const_ready = sem("const_ready")
        tok_loaded = sem("tok_loaded")
        tables_loaded = sem("tables_loaded")
        wqkv_loaded = sem("wqkv_loaded")
        wout_loaded = sem("wout_loaded")
        ffn_loaded = sem("ffn_loaded")
        setup_dve = sem("setup_dve")
        setup_pe = sem("setup_pe")
        setup_act = sem("setup_act")
        setup_pool = sem("setup_pool")
        one_hot_ready = sem("one_hot_ready")
        xhat_aggr = sem("xhat_aggr")
        h_mm = sem("h_mm")
        h_ready = sem("h_ready")
        stat_done = sem("stat_done")
        rstd_done = sem("rstd_done")
        xhat_done = sem("xhat_done")
        bias_added = sem("bias_added")
        xt_mm = sem("xt_mm")
        xt_done = sem("xt_done")
        v_mm = sem("v_mm")
        v_hi_done = sem("v_hi_done")
        v_lo_done = sem("v_lo_done")
        w_loaded = [sem(f"w_loaded{i}") for i in range(2)]
        vs_loaded = [sem(f"vs_loaded{i}") for i in range(2)]
        prj_mm = sem("prj_mm")
        prj_hi = sem("prj_hi")
        prj_lo = sem("prj_lo")
        scores_ready = sem("scores_ready")
        max_done = sem("max_done")
        exp_done = sem("exp_done")
        recip_done = sem("recip_done")
        norm_done = sem("norm_done")
        pt_ready = sem("pt_ready")
        hi_done = sem("hi_done")
        lo_done = sem("lo_done")
        pv_done = sem("pv_done")
        o_done = sem("o_done")
        y_mm = sem("y_mm")
        res_done = sem("res_done")
        stat2_done = sem("stat2_done")
        xhat2_done = sem("xhat2_done")
        x2_kept = sem("x2_kept")
        x2t_mm = sem("x2t_mm")
        x2t_done = sem("x2t_done")
        perm_zero = sem("perm_zero")
        logit_mm = sem("logit_mm")
        choose = sem("choose")
        x2_hi_done = sem("x2_hi_done")
        x2_lo_done = sem("x2_lo_done")
        permt_mm = sem("permt_mm")
        spread_done = sem("spread_done")
        taken_mm = sem("taken_mm")
        taken_done = sem("taken_done")
        hid_mm = sem("hid_mm")
        hid_done = sem("hid_done")
        int_mm = sem("int_mm")
        int_done = sem("int_done")
        intp_mm = sem("intp_mm")
        intp_done = sem("intp_done")
        res_mm = sem("res_mm")
        result_done = sem("result_done")
        stored = sem("stored")

        N_CONST = 14

        def loads(b, h, slot):
            return 16 * (H // 2) * b + 8 * (h - slot) + 16


        def wait_apart(engine, semaphore, value):
            engine.wait_ge(semaphore, value)
            engine.sem_inc(wait_passed, 1)

        block = ctx.enter_context(nc.Block())

        @block.gpsimd
        def _(pool):
            count = [0]

            def const(ins, wait=0):
                ins.then_inc(const_ready, 1)
                count[0] += 1
                return count[0]

            const(pool.memset(ones[:, :], 1.0))
            const(pool.memset(ident[:, :], 0.0))
            const(pool.memset(ident_b[:, :], 0.0))
            const(pool.memset(neg_diag[:, :], 0.0))
            const(pool.iota(vocab_id[:, :], [[0, 1]], base=0, channel_multiplier=1,
                            allow_small_or_imprecise_dtypes=True))
            const(pool.iota(tie[:, :], [[1, GROUP]], base=0, channel_multiplier=0,
                            allow_small_or_imprecise_dtypes=True))
            const(pool.memset(powers[:, 0:2 * NT], -0.5))
            const(pool.memset(powers[:, 2 * NT:3 * NT], 0.5))
            pool.wait_ge(const_ready, count[0])
            for m, fill in ((ident, 1.0), (ident_b, 1.0), (neg_diag, NEG)):
                const(pool.affine_select(out=m[:, :], in_=m[:, :], compare_op=ALU.not_equal, fill=fill,
                                         base=0, pattern=[[-1, P]], channel_multiplier=1))
            const(pool.affine_select(out=quad[:, :], in_=ones[:, 0:4], compare_op=ALU.is_ge, fill=0.0,
                                     base=0, pattern=[[-32, 4]], channel_multiplier=1))
            pool.wait_ge(const_ready, count[0])
            const(pool.affine_select(out=quad[:, :], in_=quad[:, :], compare_op=ALU.is_ge, fill=0.0,
                                     base=31, pattern=[[32, 4]], channel_multiplier=-1))
            const(pool.tensor_scalar(tie[:, :], tie[:, :], TIE, 1.0, ALU.mult, ALU.mult))
            assert count[0] == N_CONST
            pool.wait_ge(setup_dve, 2)
            pool.partition_all_reduce(qs[:, 1:2], qs[:, 0:1], P, MAX_OVER_PARTITIONS).then_inc(setup_pool, 1)
            pool.wait_ge(setup_dve, SETUP_RATIO)
            pool.tensor_tensor(norm_sb[:, 26:28], norm_sb[:, 24:26], powers[:, 2 * NT:2 * NT + 2],
                               ALU.pow).then_inc(setup_pool, 1)

            with pool.Fori(0, B) as b:
                pool.wait_ge(stat_done, 9 * (b + 1))
                pool.tensor_tensor(rstd[:, :], rstd[:, :], powers[:, 0:NT], ALU.pow).then_inc(rstd_done, 1)
                pool.wait_ge(xhat_done, NT * (b + 1))
                for t in range(NT):
                    pool.tensor_tensor(h_sb[:, b * NT + t, :], h_sb[:, b * NT + t, :], b_sb[:, :],
                                       ALU.add).then_inc(bias_added, 1)

                def divide(h):
                    for t in range(SPH):
                        n = b * SPB + h * SPH + t
                        wait_apart(pool, recip_done, n + 1)
                        pool.tensor_scalar(probs[:, t % 4, :], probs[:, t % 4, :], inv_sum[:, t % 4:t % 4 + 1],
                                           1.0, ALU.mult, ALU.mult).then_inc(norm_done, 1)

                with pool.Fori(0, H) as h:
                    divide(h)
                pool.wait_ge(stat2_done, 9 * (b + 1))
                pool.tensor_tensor(rstd[:, :], rstd[:, :], powers[:, 0:NT], ALU.pow).then_inc(rstd_done, 1)
                pool.wait_ge(xhat2_done, NT * (b + 1))
                for t in range(NT):
                    pool.tensor_copy(x2[:, b * NT + t, :], x_hat2[:, t, :]).then_inc(x2_kept, 1)

            pool.wait_ge(logit_mm, 1)
            pool.memset(perm, 0.0).then_inc(perm_zero, 1)
            for j in range(4):
                tiles = slice(4 * j, 4 * j + 4)
                if j == 0:
                    pool.wait_ge(x2_kept, TILES)
                    pool.wait_ge(pv_done, B * CPB)
                pool.tensor_copy(x2_hi[:, tiles, :], x2[:, tiles, :]).then_inc(x2_hi_done, 1)
                pool.wait_ge(x2_hi_done, j + 1)
                pool.tensor_tensor(x2_lo[:, tiles, :], x2[:, tiles, :], x2_hi[:, tiles, :].bitcast(F32),
                                   ALU.subtract).then_inc(x2_lo_done, 1)

        @block.sync
        def _(sp):
            sp.dma_start(emb_sb[0:VOCAB, :], emb).then_inc(tables_loaded, 16)
            sp.dma_start(conv_sb[0:VOCAB, :, :].rearrange("p k d -> p (k d)"),
                         conv.rearrange("(o k) d -> o (k d)", o=1).partition_broadcast(VOCAB)
                         ).then_inc(tables_loaded, 16)
            sp.dma_start(wt_sb, wqkv_t).then_inc(wqkv_loaded, 16)
            sp.dma_start(wr_sb, wqkv_rows).then_inc(wqkv_loaded, 16)
            sp.dma_start(u_sb[:, :], u_qkv).then_inc(wqkv_loaded, 16)
            sp.dma_start(wo_sb[:, :, :], wo_dup).then_inc(wout_loaded, 16)
            sp.dma_start(wor_sb, wo_rows).then_inc(wout_loaded, 16)
            sp.dma_start(uo_sb[:, :], u_out).then_inc(wout_loaded, 16)
            for i, s in enumerate((sigma_qkv, sigma_out, temperature)):
                sp.dma_start(sig[:, i:i + 1], s.partition_broadcast(P)).then_inc(wout_loaded, 16)
            sp.dma_start(wv_sb[:, :], wv).then_inc(wout_loaded, 16)
            sp.dma_start(b_sb[:, :], b_out.partition_broadcast(P)).then_inc(wout_loaded, 16)
            sp.dma_start(ctrl_sb[:, :], controller).then_inc(ffn_loaded, 16)
            sp.dma_start(f1_sb[:, :], f1).then_inc(ffn_loaded, 16)
            sp.dma_start(f2_sb[:, :, :], f2).then_inc(ffn_loaded, 16)

            def head_loads(b, h, slot, first):
                head = b * H + h
                if not first:
                    sp.wait_ge(prj_mm, 4 * (head - 1))
                sp.dma_start(w_slot[:, slot, :], w_heads[h, :, :]).then_inc(w_loaded[slot], 16)
                if first and slot == 0:
                    sp.wait_ge(v_lo_done, NT * (b + 1))
                if not first:
                    sp.wait_ge(pv_done, CPH * (head - 1))
                sp.dma_start(v_slot[:, slot, :, :].bitcast(F32), v_all[:, :, h, :].bitcast(F32)).then_inc(vs_loaded[slot], 16)

            with sp.Fori(0, B) as b:
                sp.wait_ge(batch_free, b + 1)
                sp.dma_start(tok_sb, tok[bass.ds(b, 1), :].partition_broadcast(VOCAB)).then_inc(tok_loaded, 16)
                head_loads(b, 0, 0, True)
                head_loads(b, 1, 1, True)
                with sp.Fori(0, H // 2 - 1) as p:
                    head_loads(b, 2 * p + 2, 0, False)
                    head_loads(b, 2 * p + 3, 1, False)

            for t in range(TILES):
                sp.wait_ge(result_done, t + 1)
                sp.dma_start(out[t * P:(t + 1) * P, :], result[:, t, :]).then_inc(stored, 16)
            sp.wait_ge(stored, 16 * TILES)

        @block.tensor
        def _(pe):
            pe.wait_ge(wqkv_loaded, 48)
            for t in range(12):
                last = pe.matmul(ps[:, 0, t:t + 1], wt_sb[:, t * P:(t + 1) * P], u_sb[:, :],
                                 start=True, stop=True)
            last.then_inc(setup_pe, 1)
            pe.wait_ge(wout_loaded, 16 * 8)
            for h in range(H):
                last = pe.matmul(ps[:, 1, 0:1], wo_sb[0:DH, h, :], uo_sb[:, h:h + 1],
                                 start=h == 0, stop=h == H - 1)
            last.then_inc(setup_pe, 1)
            pe.wait_ge(setup_act, 1)
            for t in range(12):
                last = pe.matmul(ps[:, 2, 0:1], wr_sb[:, t, :], norm_sb[:, t:t + 1],
                                 start=t == 0, stop=t == 11)
            last.then_inc(setup_pe, 1)
            pe.wait_ge(setup_act, 2)
            for t in range(4):
                last = pe.matmul(ps[:, 3, t:t + 1], wor_sb[:, t * P:(t + 1) * P], norm_sb[:, 12:13],
                                 start=True, stop=True)
            last.then_inc(setup_pe, 1)
            pe.wait_ge(setup_dve, SETUP_SQUARES)
            pe.wait_ge(const_ready, N_CONST)
            pe.matmul(ps[:, 7, 0:4], ones[:, :], norm_sb[:, 18:22], start=True, stop=True).then_inc(setup_pe, 1)

            def project(b, h, slot, j, first=False):
                which, c = j // 2, j % 2
                head = b * H + h
                if j == 0:
                    pe.wait_ge(w_loaded[slot], loads(b, h, slot))
                if not (first and j == 0):
                    pe.wait_ge(prj_lo, 4 * head + j)
                pe.matmul(ps[:, WORK, :], w_slot[:, slot, which * P:(which + 1) * P],
                          xt[:, c * HALF:(c + 1) * HALF], start=True, stop=True).then_inc(prj_mm, 1)

            def step(b, h, t, slot, first, last):
                n = b * SPB + h * SPH + t
                if t < SPH and not last == "drain":
                    if t == 0:
                        pe.wait_ge(prj_lo, 4 * (b * H + h + 1))
                    if not (first and t < 2):
                        pe.wait_ge(exp_done, n - 1)
                    for c in range(2):
                        bank = ps[:, SCORES + 2 * (t % 2) + c, :]
                        q = q_st[:, slot, t * P:(t + 1) * P]
                        half = slice(c * HALF, (c + 1) * HALF)
                        pe.matmul(bank, q, k_hi[:, slot, half], start=True, stop=False)
                        if c == t // 4:
                            pe.matmul(bank[:, (t % 4) * P:(t % 4 + 1) * P], neg_diag[:, :], ident_b[:, :],
                                      start=False, stop=False)
                        ins = pe.matmul(bank, q, k_lo[:, slot, half], start=False, stop=True)
                    ins.then_inc(scores_ready, 1)

                def transposes(a):
                    m = n - T_LAG
                    if a == 0:
                        pe.wait_ge(norm_done, m + 1)
                    if not (first and t == T_LAG):
                        pe.wait_ge(lo_done, 2 * m - 1 + a)
                    for q in range(4):
                        col = (4 * a + q) * P
                        ins = pe.transpose(ps[:, TRANS + a, q * P:(q + 1) * P],
                                           probs[:, (t - T_LAG) % 4, col:col + P], ident[:, :])
                    ins.then_inc(pt_ready, 1)

                def values(part):
                    c_local = (t - PV_LAG) // 2 if t % 2 else (t - PV_LAG - 1) // 2
                    c = b * CPB + h * CPH + c_local
                    vs = slot if c_local >= 0 else 1 - slot
                    buf = c_local % 2
                    if t % 2 and part == 0:
                        pe.wait_ge(lo_done, 4 * c + 4)
                        if not (first and c_local == 0):
                            pe.wait_ge(o_done, c)
                        if c_local % CPH == 0:
                            pe.wait_ge(vs_loaded[vs], loads(b, h, vs))
                    start = (0 if t % 2 else 4) + 2 * part
                    for jt in (start, start + 1):
                        for src in (pt_hi, pt_lo):
                            ins = pe.matmul(ps[:, PV_BANK, 0:CW], v_slot[:, vs, jt, :], src[:, buf, jt, :],
                                            start=jt == 0 and src is pt_hi, stop=jt == NT - 1 and src is pt_lo)
                    if jt == NT - 1:
                        ins.then_inc(pv_done, 1)

                tr = not (first and t < T_LAG) and not (last == "drain" and t >= T_LAG)
                pv = not (first and t < PV_LAG + (t % 2 == 0)) and not (last == "drain" and t >= PV_LAG)
                if tr:
                    transposes(0)
                if pv:
                    values(0)
                if tr:
                    transposes(1)
                if pv:
                    values(1)
                if not last and t % 2 == 0:
                    project(b, h + 1, 1 - slot, t // 2)

            with pe.Fori(0, B) as b:
                for t in range(NT):
                    if t == 0:
                        pe.wait_ge(setup_dve, SETUP_TABLES)
                        pe.wait_ge(setup_dve, SETUP_RATIO)
                        pe.wait_ge(one_hot_ready, 2 * (b + 1))
                    dst = ps[:, t // 4, (t % 4) * P:(t % 4 + 1) * P]
                    pe.matmul(dst, one_hot[:, t * P:(t + 1) * P], table[0:VOCAB, 0, :], start=True, stop=False)
                    ins = pe.matmul(dst, one_hot[:, 1 + t * P:1 + (t + 1) * P], table[0:VOCAB, 1, :],
                                    start=False, stop=True)
                    if t % 4 == 3:
                        ins.then_inc(h_mm, 1)
                for t in range(NT):
                    pe.wait_ge(xhat_done, NT * b + t + 1)
                    ins = pe.transpose(ps[:, 2 + t // 4, (t % 4) * P:(t % 4 + 1) * P], x_hat[:, t, :], ident[:, :])
                    if t % 4 == 3:
                        ins.then_inc(xt_mm, 1)
                pe.wait_ge(xt_done, 2 * (b + 1))
                for t in range(NT):
                    if t >= 2:
                        pe.wait_ge(v_lo_done, NT * b + t - 1)
                    pe.matmul(ps[:, t % 2, :], xt[:, t * P:(t + 1) * P], wv_sb[:, :],
                              start=True, stop=True).then_inc(v_mm, 1)
                for j in range(4):
                    project(b, 0, 0, j, True)
                pe.wait_ge(v_lo_done, NT * (b + 1))

                for t in range(SPH):
                    step(b, 0, t, 0, True, False)
                with pe.Fori(0, H // 2 - 1) as p:
                    for k in (1, 2):
                        for t in range(SPH):
                            step(b, 2 * p + k, t, k % 2, False, False)
                for t in range(SPH):
                    step(b, H - 1, t, 1, False, True)
                for t in range(PV_LAG):
                    step(b, H, t, 0, False, "drain")

                pe.wait_ge(o_done, CPB * (b + 1))
                for t in range(NT):
                    if t >= 4:
                        pe.wait_ge(res_done, NT * b + t - 3)
                    for h in range(H):
                        ins = pe.matmul(ps[:, t % 4, 0:D], o_t[:, h, t * P:(t + 1) * P], wo_sb[:, h, :],
                                        start=h == 0, stop=h == H - 1)
                    ins.then_inc(y_mm, 1)
                for t in range(NT):
                    pe.wait_ge(xhat2_done, NT * b + t + 1)
                    ins = pe.transpose(ps[:, 4 + t // 4, (t % 4) * P:(t % 4 + 1) * P], x_hat2[:, t, :], ident[:, :])
                    if t % 4 == 3:
                        ins.then_inc(x2t_mm, 1)

            pe.wait_ge(ffn_loaded, 48)
            pe.wait_ge(x2t_done, 2 * B)
            x2_pairs = x2t[:, :].rearrange("p (j u t) -> p j u t", u=2, t=GROUP)
            for c in range(2):
                for u in range(2):
                    ins = pe.matmul(ps[u * ES:(u + 1) * ES, c, :], ctrl_sb[:, :],
                                    x2_pairs[:, c * PAIRS // 2:(c + 1) * PAIRS // 2, u, :], start=True, stop=True)
            ins.then_inc(logit_mm, 1)
            pe.wait_ge(choose, 4)
            perm_flat = x2t[:, :]

            def perm_t(i):
                if i >= 2:
                    pe.wait_ge(spread_done, i - 1)
                pe.transpose(ps[:, 4 + i % 2, 0:P], perm_flat[:, i * P:(i + 1) * P], ident[:, :]).then_inc(permt_mm, 1)

            perm_t(0)
            for i in range(TILES):
                if i + 1 < TILES:
                    perm_t(i + 1)
                if i % 4 == 0:
                    pe.wait_ge(x2_lo_done, i // 4 + 1)
                pe.wait_ge(spread_done, i + 1)
                if i >= 2:
                    pe.wait_ge(taken_done, i - 1)
                mov = spread[:, i % 2, :, :]
                pe.matmul(ps[:, 2 + i % 2, :], x2_hi[:, i, :], mov, start=True, stop=False)
                pe.matmul(ps[:, 2 + i % 2, :], x2_lo[:, i, :], mov, start=False, stop=True).then_inc(taken_mm, 1)
            pe.wait_ge(taken_done, TILES)
            for k in range(NK):
                for q in range(4):
                    e = 4 * k + q
                    ins = pe.matmul(ps[32 * q:32 * (q + 1), k // 4, (k % 4) * GROUPS:(k % 4 + 1) * GROUPS],
                                    f1_sb[:, e * F:(e + 1) * F], taken[:, e, :], start=True, stop=True,
                                    tile_position=(0, 32 * q))
                if k % 4 == 3:
                    ins.then_inc(hid_mm, 1)
            for k in range(NK):
                pe.wait_ge(hid_done, k + 1)
                if k >= 2:
                    pe.wait_ge(int_done, k - 1)
                pe.matmul(ps[:, 4 + k % 2, :], f2_sb[:, k, :], hidden[:, k % 2, :],
                          start=True, stop=True).then_inc(int_mm, 1)
            pe.wait_ge(int_done, NK)

            def pair_transposes(i):
                if i >= 2:
                    pe.wait_ge(intp_done, i - 1)
                for j in range(PPT):
                    ins = pe.transpose(ps[:, 6 + i % 2, j * P:(j + 1) * P], inter_t[:, PPT * i + j, :], ident[:, :])
                ins.then_inc(intp_mm, 1)

            pair_transposes(0)
            for i in range(TILES):
                if i + 1 < TILES:
                    pair_transposes(i + 1)
                pe.wait_ge(intp_done, i + 1)
                if i >= 4:
                    pe.wait_ge(result_done, i - 3)
                for j in range(PPT):
                    ins = pe.matmul(ps[32 * j:32 * (j + 1), i % 4, 0:D], perm[:, PPT * i + j, :],
                                    inter_p[:, PPT * i + j, :], start=True, stop=True, tile_position=(0, 32 * j))
                ins.then_inc(res_mm, 1)

        @block.scalar
        def _(act):
            act.sem_inc(batch_free, 1)
            act.wait_ge(setup_pe, 1)
            act.activation(norm_sb[:, 0:12], ps[:, 0, 0:12], ACT.Copy).then_inc(setup_act, 1)
            act.wait_ge(setup_pe, 2)
            act.activation(norm_sb[:, 12:13], ps[:, 1, 0:1], ACT.Copy).then_inc(setup_act, 1)
            act.wait_ge(setup_pe, 3)
            act.activation(norm_sb[:, 13:14], ps[:, 2, 0:1], ACT.Copy).then_inc(setup_act, 1)
            act.wait_ge(setup_pe, 4)
            act.activation(norm_sb[:, 14:18], ps[:, 3, 0:4], ACT.Copy).then_inc(setup_act, 1)
            act.wait_ge(wout_loaded, 16 * 8)
            act.activation(norm_sb[:, 28:29], sig[:, 2:3], ACT.Exp).then_inc(setup_act, 1)

            q_scale, v_scale = norm_sb[:, 31:32], norm_sb[:, 29:30]

            def project_hi(b, head, slot, j):
                which, c = j // 2, j % 2
                act.wait_ge(prj_mm, 4 * head + j + 1)
                half = slice(c * HALF, (c + 1) * HALF)
                if which == 0:
                    ins = act.activation(q_st[:, slot, half], ps[:, WORK, :], ACT.Copy, scale=q_scale)
                else:
                    ins = act.activation(k_hi[:, slot, half], ps[:, WORK, :], ACT.Copy)
                ins.then_inc(prj_hi, 1)

            def step(b, h, t, slot, first, last):
                n = b * SPB + h * SPH + t

                def high(a):
                    m = n - T_LAG
                    m_local = (t - T_LAG) % SPH
                    chunk = b * CPB + h * CPH + (t - T_LAG) // 2
                    act.wait_ge(pt_ready, 2 * m + a + 1)
                    if a == 0 and not (first and t - T_LAG < 4):
                        act.wait_ge(pv_done, chunk - 1)
                    dst = pt_hi[:, m_local // 2 % 2, 4 * a:4 * a + 4, (m_local % 2) * P:(m_local % 2 + 1) * P]
                    act.activation(dst, ps[:, TRANS + a, :].rearrange("p (j c) -> p j c", c=P),
                                   ACT.Copy).then_inc(hi_done, 1)

                if not last and t % 2:
                    if t == 1 and not first:
                        act.wait_ge(scores_ready, n - 1)
                    project_hi(b, b * H + h + 1, 1 - slot, t // 2)
                if t % 2 and not (first and t < PV_LAG + 2):
                    c_local = (t - PV_LAG - 2) // 2
                    c = b * CPB + h * CPH + c_local
                    head = h if c_local >= 0 else h - 1
                    cols = slice((c_local % CPH) * CW, (c_local % CPH + 1) * CW)
                    act.wait_ge(pv_done, c + 1)
                    act.activation(o_t[:, head, cols], ps[:, PV_BANK, 0:CW], ACT.Copy).then_inc(o_done, 1)
                tr = not (first and t < T_LAG) and not (last == "drain" and t >= T_LAG)
                if tr:
                    high(0)
                    high(1)
                if last != "drain":
                    act.wait_ge(max_done, n + 1)
                    if not (first and t < 4):
                        act.wait_ge(pt_ready, 2 * n - 6)
                    act.activation(probs[:, t % 4, :].rearrange("p (a c) -> p a c", a=2),
                                   ps[:, SCORES + 2 * (t % 2):SCORES + 2 * (t % 2) + 2, :], ACT.Exp,
                                   bias=neg_max[:, t % 4:t % 4 + 1],
                                   accum_out=row_sum[:, t % 4:t % 4 + 1]).then_inc(exp_done, 1)

            with act.Fori(0, B) as b:
                for c in range(2):
                    act.wait_ge(h_mm, 2 * b + c + 1)
                    act.activation(h_sb[:, bass.ds(b * NT + 4 * c, 4), :],
                                   ps[:, c, :].rearrange("p (t d) -> p t d", d=D), ACT.Relu).then_inc(h_ready, 1)
                for c in range(2):
                    act.wait_ge(xt_mm, 2 * b + c + 1)
                    act.activation(xt[:, c * HALF:(c + 1) * HALF], ps[:, 2 + c, :], ACT.Copy).then_inc(xt_done, 1)
                act.wait_ge(setup_dve, SETUP_SCALES)
                for t in range(NT):
                    act.wait_ge(v_mm, NT * b + t + 1)
                    act.activation(v_all[:, t, :, 0:DH], ps[:, t % 2, :].rearrange("p (h c) -> p h c", c=DH),
                                   ACT.Copy, scale=v_scale).then_inc(v_hi_done, 1)
                for j in range(4):
                    project_hi(b, b * H, 0, j)

                for t in range(SPH):
                    step(b, 0, t, 0, True, False)
                with act.Fori(0, H // 2 - 1) as p:
                    for k in (1, 2):
                        for t in range(SPH):
                            step(b, 2 * p + k, t, k % 2, False, False)
                for t in range(SPH):
                    step(b, H - 1, t, 1, False, True)
                for t in range(PV_LAG + 1):
                    step(b, H, t, 0, False, "drain")

                for c in range(2):
                    act.wait_ge(x2t_mm, 2 * b + c + 1)
                    act.activation(x2t[:, bass.ds(b * SEQ + c * HALF, HALF)], ps[:, 4 + c, :],
                                   ACT.Copy).then_inc(x2t_done, 1)
                act.wait_ge(x2t_done, 2 * (b + 1))
                act.sem_inc(batch_free, 1)

            for i in range(TILES):
                act.wait_ge(taken_mm, i + 1)
                act.activation(taken[:, :, 8 * i:8 * i + 8].rearrange("p e g -> p g e"),
                               ps[:, 2 + i % 2, :].rearrange("p (g e) -> p g e", e=ES),
                               ACT.Copy).then_inc(taken_done, 1)
            act.wait_ge(hid_mm, 4)
            inter_v = inter_t.rearrange("p j (u e) -> p e j u", u=2)
            for k in range(NK):
                act.wait_ge(int_mm, k + 1)
                act.activation(inter_v[:, 4 * k:4 * k + 4, :, :],
                               ps[:, 4 + k % 2, :].rearrange("p (q j u) -> p q j u", q=4, u=2),
                               ACT.Copy).then_inc(int_done, 1)
            for i in range(TILES):
                act.wait_ge(intp_mm, i + 1)
                act.activation(inter_p[:, PPT * i:PPT * (i + 1), :],
                               ps[:, 6 + i % 2, :].rearrange("p (j d) -> p j d", d=D), ACT.Copy).then_inc(intp_done, 1)

        @block.vector
        def _(dve):
            count = [0]

            def link(ins):
                count[0] += 1
                ins.then_inc(setup_dve, 1)
                dve.wait_ge(setup_dve, count[0])

            link(dve.memset(qs[:, :], 0.0))
            dve.wait_ge(tables_loaded, 32)
            link(dve.tensor_reduce(qs[0:VOCAB, 0:1], emb_sb[0:VOCAB, :], AXX, ALU.max, apply_absolute_value=True))
            link(dve.tensor_reduce(qs[0:VOCAB, 2:3], conv_sb[0:VOCAB, :, :].rearrange("p k d -> p (k d)"), AXX,
                                   ALU.max, apply_absolute_value=True))
            dve.wait_ge(setup_pool, 1)
            link(dve.tensor_scalar(qs[0:VOCAB, 3:5], qs[0:VOCAB, 1:3], 1.0 / QMAX, None, ALU.mult))
            link(dve.reciprocal(qs[0:VOCAB, 5:7], qs[0:VOCAB, 3:5]))
            parts = [(emb_sb[0:VOCAB, :], quant[0:VOCAB, 0:D], 0),
                     (conv_sb[0:VOCAB, :, :].rearrange("p k d -> p (k d)"), quant[0:VOCAB, D:3 * D], 1)]
            for w, q, i in parts:
                link(dve.tensor_scalar(q, w, qs[0:VOCAB, 5 + i:6 + i], ROUND, ALU.mult, ALU.add))
                link(dve.tensor_scalar(q, q, ROUND, qs[0:VOCAB, 3 + i:4 + i], ALU.subtract, ALU.mult))
                link(dve.tensor_tensor(q, q, w, ALU.subtract))
                link(dve.tensor_tensor(q, w, q, ALU.add))
            for k in range(2):
                link(dve.tensor_tensor(table[0:VOCAB, k, :], quant[0:VOCAB, 0:D],
                                       quant[0:VOCAB, D * (k + 1):D * (k + 2)], ALU.mult))
            assert count[0] == SETUP_TABLES
            dve.wait_ge(setup_act, 4)
            sq = norm_sb[:, 22:24]
            scratch = quant[:, 0:12]
            for a, n, col in ((0, 12, 18), (12, 1, 19), (13, 1, 20), (14, 4, 21)):
                v = norm_sb[:, a:a + n]
                link(dve.tensor_tensor(scratch[:, 0:n], v, v, ALU.mult))
                link(dve.tensor_reduce(norm_sb[:, col:col + 1], scratch[:, 0:n], AXX, ALU.add))
            assert count[0] == SETUP_SQUARES
            dve.wait_ge(setup_pe, 5)
            link(dve.reciprocal(sq, ps[:, 7, 2:4]))
            link(dve.tensor_tensor(norm_sb[:, 24:26], ps[:, 7, 0:2], sq, ALU.mult))
            assert count[0] == SETUP_RATIO
            dve.wait_ge(setup_pool, 2)
            dve.wait_ge(wout_loaded, 16 * 8)
            dve.wait_ge(setup_act, 5)
            link(dve.tensor_tensor(norm_sb[:, 29:31], norm_sb[:, 26:28], sig[:, 0:2], ALU.mult))
            link(dve.scalar_tensor_tensor(norm_sb[:, 31:32], norm_sb[:, 29:30], norm_sb[:, 28:29],
                                          norm_sb[:, 29:30], ALU.mult, ALU.mult))
            assert count[0] == SETUP_SCALES
            q_scale, v_scale, o_scale = norm_sb[:, 31:32], norm_sb[:, 29:30], norm_sb[:, 30:31]
            dve.wait_ge(const_ready, N_CONST)

            def project_lo(b, head, slot, j):
                which, c = j // 2, j % 2
                half = slice(c * HALF, (c + 1) * HALF)
                dve.wait_ge(prj_hi, 4 * head + j + 1)
                if which == 0:
                    low = q_st[DH:P, slot, half]
                    ins = dve.scalar_tensor_tensor(low, ps[DH:P, WORK, :], norm_sb[DH:P, 31:32],
                                                   low.bitcast(F32), ALU.mult, ALU.subtract)
                else:
                    ins = dve.tensor_tensor(k_lo[:, slot, half], ps[:, WORK, :],
                                            k_hi[:, slot, half].bitcast(F32), ALU.subtract)
                ins.then_inc(prj_lo, 1)

            def step(b, h, t, slot, first, last):
                n = b * SPB + h * SPH + t

                def low(a):
                    m = n - T_LAG
                    m_local = (t - T_LAG) % SPH
                    at = (slice(None), m_local // 2 % 2, slice(4 * a, 4 * a + 4),
                          slice((m_local % 2) * P, (m_local % 2 + 1) * P))
                    dve.wait_ge(hi_done, 2 * m + a + 1)
                    dve.tensor_tensor(pt_lo[at], ps[:, TRANS + a, :].rearrange("p (j c) -> p j c", c=P),
                                      pt_hi[at].bitcast(F32), ALU.subtract).then_inc(lo_done, 1)

                tr = not (first and t < T_LAG) and not (last == "drain" and t >= T_LAG)
                if not (first and t == 0) and not (last == "drain" and t > 0):
                    dve.wait_ge(exp_done, n)
                    dve.reciprocal(inv_sum[:, (t - 1) % 4:(t - 1) % 4 + 1],
                                   row_sum[:, (t - 1) % 4:(t - 1) % 4 + 1]).then_inc(recip_done, 1)
                if last != "drain":
                    dve.wait_ge(scores_ready, n + 1)
                    dve.tensor_reduce(neg_max[:, t % 4:t % 4 + 1],
                                      ps[:, SCORES + 2 * (t % 2):SCORES + 2 * (t % 2) + 2, :].rearrange(
                                          "p a c -> p (a c)"),
                                      AXX, ALU.max, negate=True).then_inc(max_done, 1)
                if tr:
                    low(0)
                if tr:
                    low(1)
                if not last and t % 2:
                    project_lo(b, b * H + h + 1, 1 - slot, t // 2)

            with dve.Fori(0, B) as b:
                dve.wait_ge(tok_loaded, 16 * (b + 1))
                dve.memset(one_hot[:, 0:1], 0.0).then_inc(one_hot_ready, 1)
                dve.tensor_scalar(one_hot[:, 1:SEQ + 1], tok_sb, float(VOCAB - 1), vocab_id[0:VOCAB, :],
                                  ALU.min, ALU.is_equal).then_inc(one_hot_ready, 1)
                for t in range(NT):
                    wait_apart(dve, h_ready, 2 * b + t // 4 + 1)
                    dve.bn_stats(stats[:, t, :], h_sb[:, b * NT + t, :]).then_inc(stat_done, 1)
                for t in range(NT):
                    wait_apart(dve, stat_done, 9 * b + t + 1)
                    ins = dve.bn_aggr(mv[:, t, :], stats[:, t, :])
                ins.then_inc(xhat_aggr, 1)
                dve.wait_ge(xhat_aggr, 2 * b + 1)
                dve.tensor_scalar(rstd[:, :], mv[:, :, 1], EPS, None, ALU.add).then_inc(stat_done, 1)
                dve.wait_ge(rstd_done, 2 * b + 1)
                for t in range(NT):
                    dve.tensor_scalar(x_hat[:, t, :], h_sb[:, b * NT + t, :], mv[:, t, 0:1], rstd[:, t:t + 1],
                                      ALU.subtract, ALU.mult).then_inc(xhat_done, 1)
                for t in range(NT):
                    dve.wait_ge(v_hi_done, NT * b + t + 1)
                    dve.scalar_tensor_tensor(v_all[:, t, :, DH:P], ps[:, t % 2, :].rearrange(
                        "p (h c) -> p h c", c=DH), v_scale, v_all[:, t, :, 0:DH].bitcast(F32),
                        ALU.mult, ALU.subtract).then_inc(v_lo_done, 1)
                for j in range(4):
                    project_lo(b, b * H, 0, j)

                for t in range(SPH):
                    step(b, 0, t, 0, True, False)
                with dve.Fori(0, H // 2 - 1) as p:
                    for k in (1, 2):
                        for t in range(SPH):
                            step(b, 2 * p + k, t, k % 2, False, False)
                for t in range(SPH):
                    step(b, H - 1, t, 1, False, True)
                for t in range(T_LAG):
                    step(b, H, t, 0, False, "drain")

                dve.wait_ge(bias_added, NT * (b + 1))
                for t in range(NT):
                    dve.wait_ge(y_mm, NT * b + t + 1)
                    tile = h_sb[:, b * NT + t, :]
                    dve.scalar_tensor_tensor(tile, ps[:, t % 4, 0:D], o_scale, tile,
                                             ALU.mult, ALU.add).then_inc(res_done, 1)
                for t in range(NT):
                    wait_apart(dve, res_done, NT * b + t + 1)
                    dve.bn_stats(stats[:, t, :], h_sb[:, b * NT + t, :]).then_inc(stat2_done, 1)
                for t in range(NT):
                    wait_apart(dve, stat2_done, 9 * b + t + 1)
                    ins = dve.bn_aggr(mv[:, t, :], stats[:, t, :])
                ins.then_inc(xhat_aggr, 1)
                dve.wait_ge(xhat_aggr, 2 * b + 2)
                dve.tensor_scalar(rstd[:, :], mv[:, :, 1], EPS, None, ALU.add).then_inc(stat2_done, 1)
                dve.wait_ge(rstd_done, 2 * b + 2)
                for t in range(NT):
                    dve.tensor_scalar(x_hat2[:, t, :], h_sb[:, b * NT + t, :], mv[:, t, 0:1], rstd[:, t:t + 1],
                                      ALU.subtract, ALU.mult).then_inc(xhat2_done, 1)

            dve.wait_ge(logit_mm, 1)
            lg = logits.rearrange("p (j t) -> p j t", t=GROUP)
            dve.tensor_tensor(lg, ps[:, 0:2, :].rearrange("p c (j t) -> p (c j) t", t=GROUP),
                              tie[:, :].unsqueeze(1).broadcast_to([P, PAIRS, GROUP]), ALU.add).then_inc(choose, 1)
            dve.wait_ge(choose, 1)
            dve.tensor_reduce(group_max[:, :], lg, AXX, ALU.max).then_inc(choose, 1)
            dve.wait_ge(choose, 2)
            dve.wait_ge(perm_zero, 1)
            for u in range(2):
                rows = slice(u * ES, (u + 1) * ES)
                dve.tensor_tensor(perm[rows, :, u * GROUP:(u + 1) * GROUP], lg[rows, :, :],
                                  group_max[rows, :].unsqueeze(2).broadcast_to([ES, PAIRS, GROUP]),
                                  ALU.is_equal).then_inc(choose, 1)
            for i in range(TILES):
                dve.wait_ge(permt_mm, i + 1)
                if i >= 2:
                    dve.wait_ge(taken_mm, i - 1)
                dve.tensor_tensor(spread[:, i % 2, :, :],
                                  ps[:, 4 + i % 2, 0:P].unsqueeze(1).broadcast_to([P, 4, P]),
                                  quad[:, :].unsqueeze(2).broadcast_to([P, 4, P]), ALU.mult).then_inc(spread_done, 1)
            for k in range(NK):
                dve.wait_ge(hid_mm, k // 4 + 1)
                if k >= 2:
                    dve.wait_ge(int_mm, k - 1)
                dve.scalar_tensor_tensor(
                    hidden[:, k % 2, :].rearrange("p (q g) -> p q g", q=4),
                    ps[:, k // 4, (k % 4) * GROUPS:(k % 4 + 1) * GROUPS].unsqueeze(1).broadcast_to([P, 4, GROUPS]),
                    0.0, quad[:, :].unsqueeze(2).broadcast_to([P, 4, GROUPS]), ALU.max,
                    ALU.mult).then_inc(hid_done, 1)
            for i in range(TILES):
                dve.wait_ge(res_mm, i + 1)
                dve.tensor_tensor(result[:, i, :], ps[:, i % 4, 0:D], h_sb[:, i, :], ALU.add).then_inc(result_done, 1)


SETUP_TABLES = 15
SETUP_SQUARES = SETUP_TABLES + 8
SETUP_RATIO = SETUP_SQUARES + 2
SETUP_SCALES = SETUP_RATIO + 2


def kernel(**inputs):
    import concourse.bacc as bacc
    from concourse.bass_utils import run_bass_kernel_spmd

    a = {k: np.asarray(v) for k, v in inputs.items()}
    w = a["L0_attn_w_qkv"]
    wo = a["L0_attn_w_out"]

    def doubled(x):
        return np.concatenate([x, x], axis=2)

    heads = w.reshape(3, H, DH, D).transpose(0, 1, 3, 2)
    wo_t = wo.reshape(D, H, DH).transpose(2, 1, 0)
    arrays = {
        "tok": a["x"].astype(np.int32, copy=False),
        "emb": a["L0_tok_emb_weight"],
        "conv": a["L0_tok_conv_weight"].reshape(D, 2).T,
        "w_heads": np.concatenate([doubled(heads[0]), doubled(heads[1])], axis=2),
        "wv": w[2 * H * DH:].T,
        "wqkv_t": w.T,
        "wqkv_rows": w.reshape(12, P, D).transpose(1, 0, 2),
        "u_qkv": a["L0_attn_u_qkv"].reshape(D, 1),
        "wo_dup": np.concatenate([wo_t, wo_t], axis=0),
        "wo_rows": wo,
        "u_out": a["L0_attn_u_out"].reshape(H, DH).T,
        "sigma_qkv": a["L0_attn_sigma_qkv"].reshape(1, 1),
        "sigma_out": a["L0_attn_sigma_out"].reshape(1, 1),
        "temperature": a["L0_attn_temperature"].reshape(1, 1),
        "b_out": a["L0_attn_b_out"].reshape(1, D),
        "controller": a["L0_ffn_controller"].reshape(D, ES),
        "f1": a["L0_ffn_f1"].reshape(D, ES * F),
        "f2": a["L0_ffn_f2"].reshape(NK, P, D).transpose(1, 0, 2),
    }
    nc = bacc.Bacc("TRN2", target_bir_lowering=False, num_devices=1)
    feeds, args = {}, []
    for name, x in arrays.items():
        x = np.ascontiguousarray(x)
        feeds["in_" + name] = x
        args.append(nc.dram_tensor("in_" + name, x.shape, mybir.dt.from_np(x.dtype), kind="ExternalInput").ap())
    args.append(nc.dram_tensor("out_h", (B * SEQ, D), F32, kind="ExternalOutput").ap())
    layer_kernel(nc, *args)
    r = run_bass_kernel_spmd(nc, [feeds], core_ids=[0])
    return r.results[0]["out_h"].reshape(B, SEQ, D)
```

```python
import numpy as np
from contextlib import ExitStack

import concourse.bass as bass
from concourse import mybir

F32 = mybir.dt.float32
F32R = mybir.dt.float32r
BF16 = mybir.dt.bfloat16
I32 = mybir.dt.int32
ALU = mybir.AluOpType
ACT = mybir.ActivationFunctionType
AXX = mybir.AxisListType.X
MAX_OVER_PARTITIONS = bass.bass_isa.ReduceOp.max

P = 128
B, SEQ, D = 2, 1024, 128
VOCAB = 125
H, DH = 8, 64
NT = SEQ // P
TILES = B * NT
SPH = NT
SPB = H * SPH
CPH = NT // 2
CPB = H * CPH
CW = 2 * P
HALF = SEQ // 2
GROUP = 16
ES = 64
F = 32
PAIRS = B * SEQ // (2 * GROUP)
GROUPS = 2 * PAIRS
PPT = PAIRS // TILES
NK = ES * F // P
QMAX = 127.0
ROUND = 12582912.0
NEG = -3.0e38
EPS = 1e-5
TIE = 1e-6 / (GROUP - 1)
T_LAG, PV_LAG = 3, 5


def layer_kernel(nc, tok, emb, conv, w_pairs, wv, wqkv_t, wqkv_rows, u_qkv, wo_dup, wo_rows, u_out,
                 sigma_qkv, sigma_out, temperature, b_out, controller, f1, f2, out):
    with ExitStack() as ctx:
        def sb(name, shape, dt=F32):
            return ctx.enter_context(nc.sbuf_tensor(name, shape, dt))

        def sem(name):
            return ctx.enter_context(nc.semaphore(name))

        ps = ctx.enter_context(nc.psum_tensor("ps", [P, 8, 512], F32))
        SCORES, TRANS, PV_BANK, WORK = 0, 4, 6, 7

        ident = sb("ident", [P, P])
        ident_b = sb("ident_b", [P, P], BF16)
        neg_diag = sb("neg_diag", [P, P], BF16)
        ones = sb("ones", [P, P])
        quad = sb("quad", [P, 4])
        vocab_id = sb("vocab_id", [P, 1])
        tie = sb("tie", [P, GROUP])
        powers = sb("powers", [P, 3 * NT])
        emb_sb = sb("emb_sb", [P, D])
        conv_sb = sb("conv_sb", [P, 2, D])
        quant = sb("quant", [P, 3 * D])
        table = sb("table", [P, 2, D])
        qs = sb("qs", [P, 8])
        wv_sb = sb("wv_sb", [P, H * DH])
        wo_sb = sb("wo_sb", [P, H, D])
        u_sb = sb("u_sb", [P, 1])
        uo_sb = sb("uo_sb", [DH, H])
        sig = sb("sig", [P, 3])
        norm_sb = sb("norm_sb", [P, 32])
        w_slot = sb("w_slot", [P, 2, P])
        b_sb = sb("b_sb", [P, D])
        h_sb = sb("h_sb", [P, TILES, D])
        x2 = sb("x2", [P, TILES, D])
        x2t = sb("x2t", [P, B * SEQ])
        xt = sb("xt", [P, SEQ])
        stats = sb("stats", [P, TILES, 6])
        mv = sb("mv", [P, TILES, 2])
        rstd = sb("rstd", [P, TILES])
        q_st = sb("q_st", [P, 2, SEQ], F32R)
        k_hi = sb("k_hi", [P, 2, SEQ], F32R)
        k_lo = sb("k_lo", [P, 2, SEQ], F32R)
        v_all = sb("v_all", [P, NT, H, P], F32R)
        v_slot = sb("v_slot", [P, 2, NT, P], F32R)
        probs = sb("probs", [P, 4, SEQ])
        neg_max = sb("neg_max", [P, 4])
        row_sum = sb("row_sum", [P, 4])
        inv_sum = sb("inv_sum", [P, 4])
        pt_hi = sb("pt_hi", [P, 2, NT, CW], F32R)
        pt_lo = sb("pt_lo", [P, 2, NT, CW], F32R)
        arena = sb("arena", [P, 8 * SEQ])
        ctrl_sb = sb("ctrl_sb", [P, ES])
        f1_sb = sb("f1_sb", [P, ES * F])
        f2_sb = sb("f2_sb", [P, NK, D])
        group_max = sb("group_max", [P, PAIRS])

        probs_flat = probs[:, :, :].rearrange("p a b -> p (a b)")
        one_hot = [probs_flat[0:VOCAB, 2 * SEQ * b:2 * SEQ * b + SEQ + 1] for b in range(B)]
        x2_flat = x2[:, :, :].rearrange("p t d -> p (t d)")
        tok_sb = [x2_flat[0:VOCAB, SEQ * b:SEQ * (b + 1)].bitcast(I32) for b in range(B)]
        logits = probs_flat[:, 0:SEQ]
        hidden = probs_flat[:, SEQ:2 * SEQ].rearrange("p (r n) -> p r n", r=2)
        result = probs_flat[:, 2 * SEQ:4 * SEQ].rearrange("p (t d) -> p t d", d=D)
        perm = x2t[:, :].rearrange("p (j t) -> p j t", t=2 * GROUP)
        wt_sb = arena[:, 0:12 * P]
        wr_sb = arena[:, 12 * P:24 * P].rearrange("p (t d) -> p t d", d=D)
        wor_sb = arena[:, 24 * P:24 * P + H * DH]
        x_hat = [arena[:, (4 + 3 * b) * SEQ:(5 + 3 * b) * SEQ].rearrange("p (t d) -> p t d", d=D) for b in range(B)]
        pair_qk = arena[:, 0:4 * SEQ].rearrange("p (w l n) -> p w l n", w=2, l=2)
        o_slot = arena[:, 4 * SEQ:6 * SEQ].rearrange("p (s n) -> p s n", s=2)
        inter_p = arena[:, :].rearrange("p (j d) -> p j d", d=D)
        v_flat = v_all[:, :, :, :].rearrange("p t h c -> p (t h c)").bitcast(F32)
        taken = v_flat.rearrange("p (e g) -> p e g", g=GROUPS)
        inter_t = v_flat.rearrange("p (j r) -> p j r", r=P)
        pt_hi_flat = pt_hi[:, :, :, :].rearrange("p a t c -> p (a t c)")
        pt_lo_flat = pt_lo[:, :, :, :].rearrange("p a t c -> p (a t c)")
        spread = pt_hi_flat[:, 0:1024].rearrange("p (r j c) -> p r j c", r=2, c=P)
        x2_hi = pt_lo_flat[:, 0:2048].rearrange("p (t d) -> p t d", d=D)
        x2_lo = pt_lo_flat[:, 2048:4096].rearrange("p (t d) -> p t d", d=D)

        wait_passed = sem("wait_passed")
        const_ready = sem("const_ready")
        tok_loaded = sem("tok_loaded")
        tables_loaded = sem("tables_loaded")
        wqkv_loaded = sem("wqkv_loaded")
        wqkv_rows_loaded = sem("wqkv_rows_loaded")
        wout_loaded = sem("wout_loaded")
        attn_loaded = sem("attn_loaded")
        ffn_loaded = sem("ffn_loaded")
        setup_dve = sem("setup_dve")
        setup_pe = sem("setup_pe")
        setup_act = sem("setup_act")
        setup_pool = sem("setup_pool")
        one_hot_ready = sem("one_hot_ready")
        h_mm = sem("h_mm")
        h_ready = sem("h_ready")
        stat_done = sem("stat_done")
        setup_norm = sem("setup_norm")
        aggr_done = sem("aggr_done")
        rstd_done = sem("rstd_done")
        xhat_done = sem("xhat_done")
        bias_added = sem("bias_added")
        xt_mm = sem("xt_mm")
        xt_done = sem("xt_done")
        v_mm = sem("v_mm")
        v_hi_done = sem("v_hi_done")
        v_lo_done = sem("v_lo_done")
        w_loaded = sem("w_loaded")
        qk_loaded = [sem(f"qk_loaded{i}") for i in range(2)]
        vs_loaded = [sem(f"vs_loaded{i}") for i in range(2)]
        work_mm = sem("work_mm")
        work_hi = sem("work_hi")
        work_read = sem("work_read")
        scores_ready = sem("scores_ready")
        max_done = sem("max_done")
        exp_done = sem("exp_done")
        recip_done = sem("recip_done")
        norm_done = sem("norm_done")
        pt_ready = sem("pt_ready")
        hi_done = sem("hi_done")
        lo_done = sem("lo_done")
        pv_done = sem("pv_done")
        o_done = sem("o_done")
        x2_done = sem("x2_done")
        x2t_mm = sem("x2t_mm")
        x2t_done = sem("x2t_done")
        perm_zero = sem("perm_zero")
        logit_mm = sem("logit_mm")
        choose = sem("choose")
        x2_hi_done = sem("x2_hi_done")
        x2_lo_done = sem("x2_lo_done")
        permt_mm = sem("permt_mm")
        spread_done = sem("spread_done")
        taken_mm = sem("taken_mm")
        taken_done = sem("taken_done")
        hid_mm = sem("hid_mm")
        hid_done = sem("hid_done")
        int_mm = sem("int_mm")
        int_done = sem("int_done")
        intp_mm = sem("intp_mm")
        intp_done = sem("intp_done")
        res_mm = sem("res_mm")
        result_done = sem("result_done")
        stored = sem("stored")

        N_CONST = 14

        def wait_apart(engine, semaphore, value):
            engine.wait_ge(semaphore, value)
            engine.sem_inc(wait_passed, 1)

        Y = {(k, t): y for k in range(2) for t, y in ((4, "y0"), (6, "y1"))}
        QK = {(0, 3): "q0", (0, 5): "q1", (0, 7): "k0", (1, 1): "k1"}
        MID = {**QK, **Y}
        FIRST = {**QK, (1, 4): "y0", (1, 6): "y1"}
        SWITCH = {(0, 0): "x0", (0, 1): "x1", (0, 2): "q0", (0, 3): "q1", (0, 5): "k0", (0, 7): "k1",
                  (1, 0): "v0", (1, 1): "v1", (1, 2): "v2", (1, 3): "v3", (1, 5): "v4", (1, 7): "v5", **Y}
        AGAIN = {(0, 0): "v6", (0, 1): "v7", **MID}
        LAST = dict(Y)
        DRAIN = {(0, 3): "y0", (0, 6): "y1"}
        PAIR_WORK = [FIRST, MID, MID, SWITCH, AGAIN, MID, MID, LAST, DRAIN]

        def order(work):
            return sorted(work)

        def highs(work):
            return [x for x in order(work) if work[x][0] in "qkv"]

        USES = [4 + sum(len(w) for w in PAIR_WORK[:i]) for i in range(9)]
        HIGHS = [4 + sum(len(highs(w)) for w in PAIR_WORK[:i]) for i in range(9)]

        SETUP_QK = {"q0": WORK, "q1": 0, "k0": 1, "k1": 2}

        class Pair:

            def __init__(self, i, p=0):
                self.work, self.b, self.i = PAIR_WORK[i], i // 4, i
                self.index = p + i
                self.step0 = 2 * SPH * p + 2 * SPH * i
                self.chunk0 = 2 * CPH * p + 2 * CPH * i
                self.head_pair = p + i % 4
                self.head = 2 * p + 2 * (i % 4)
                self.uses = len(MID) * p + USES[i]
                self.highs = len(highs(MID)) * p + HIGHS[i]
                self.slot_loads = 16 * p + 16 * (i + 1)

            def use(self, k, t):
                return self.uses + order(self.work).index((k, t)) + 1

            def use_of(self, kind):
                return self.use(*next(x for x in self.work if self.work[x] == kind))

            def high(self, k, t):
                return self.highs + highs(self.work).index((k, t)) + 1

        def run_pairs(engine, pair_body):
            for first in (0, 4):
                pair_body(Pair(first))
                with engine.Fori(0, 2) as p:
                    pair_body(Pair(first + 1, p))
                pair_body(Pair(first + 3))

        block = ctx.enter_context(nc.Block())

        @block.gpsimd
        def _(pool):
            count = [0]

            def const(ins, wait=0):
                ins.then_inc(const_ready, 1)
                count[0] += 1
                return count[0]

            const(pool.memset(ones[:, :], 1.0))
            const(pool.memset(ident[:, :], 0.0))
            const(pool.memset(ident_b[:, :], 0.0))
            const(pool.memset(neg_diag[:, :], 0.0))
            const(pool.iota(vocab_id[:, :], [[0, 1]], base=0, channel_multiplier=1,
                            allow_small_or_imprecise_dtypes=True))
            const(pool.iota(tie[:, :], [[1, GROUP]], base=0, channel_multiplier=0,
                            allow_small_or_imprecise_dtypes=True))
            const(pool.memset(powers[:, 0:2 * NT], -0.5))
            const(pool.memset(powers[:, 2 * NT:3 * NT], 0.5))
            pool.wait_ge(const_ready, count[0])
            for m, fill in ((ident, 1.0), (ident_b, 1.0), (neg_diag, NEG)):
                const(pool.affine_select(out=m[:, :], in_=m[:, :], compare_op=ALU.not_equal, fill=fill,
                                         base=0, pattern=[[-1, P]], channel_multiplier=1))
            const(pool.affine_select(out=quad[:, :], in_=ones[:, 0:4], compare_op=ALU.is_ge, fill=0.0,
                                     base=0, pattern=[[-32, 4]], channel_multiplier=1))
            pool.wait_ge(const_ready, count[0])
            const(pool.affine_select(out=quad[:, :], in_=quad[:, :], compare_op=ALU.is_ge, fill=0.0,
                                     base=31, pattern=[[32, 4]], channel_multiplier=-1))
            const(pool.tensor_scalar(tie[:, :], tie[:, :], TIE, 1.0, ALU.mult, ALU.mult))
            assert count[0] == N_CONST
            pool.wait_ge(setup_dve, 2)
            pool.partition_all_reduce(qs[:, 1:2], qs[:, 0:1], P, MAX_OVER_PARTITIONS).then_inc(setup_pool, 1)
            def deviations(tiles, count):
                pool.wait_ge(aggr_done, count)
                pool.tensor_tensor(rstd[:, tiles], rstd[:, tiles], powers[:, 0:NT], ALU.pow).then_inc(rstd_done, 1)

            deviations(slice(0, NT), 1)
            pool.wait_ge(setup_dve, SETUP_RATIO)
            pool.tensor_tensor(norm_sb[:, 26:28], norm_sb[:, 24:26], powers[:, 2 * NT:2 * NT + 2],
                               ALU.pow).then_inc(setup_pool, 1)
            def add_bias(b):
                pool.wait_ge(xhat_done, NT * (b + 1))
                pool.tensor_tensor(h_sb[:, b * NT:(b + 1) * NT, :], h_sb[:, b * NT:(b + 1) * NT, :],
                                   b_sb[:, :].unsqueeze(1).broadcast_to([P, NT, D]), ALU.add).then_inc(bias_added, 1)

            pool.wait_ge(attn_loaded, 32)
            add_bias(0)

            def divide(pair):
                for k in range(2):
                    for t in range(SPH):
                        wait_apart(pool, recip_done, pair.step0 + k * SPH + t + 1)
                        pool.tensor_scalar(probs[:, t % 4, :], probs[:, t % 4, :], inv_sum[:, t % 4:t % 4 + 1],
                                           1.0, ALU.mult, ALU.mult).then_inc(norm_done, 1)
                        if (k, t) == (1, 0) and pair.i == 0:
                            deviations(slice(NT, 2 * NT), 2)
                        if (k, t) == (1, 0) and pair.i == 7:
                            deviations(slice(0, NT), 3)
                        if (k, t) == (1, 7) and pair.i == 0:
                            add_bias(1)

            run_pairs(pool, divide)
            deviations(slice(NT, 2 * NT), 4)
            pool.wait_ge(logit_mm, 1)
            pool.memset(perm, 0.0).then_inc(perm_zero, 1)
            for j in range(4):
                tiles = slice(4 * j, 4 * j + 4)
                pool.wait_ge(x2_done, 4 * j + 4)
                if j == 0:
                    pool.wait_ge(pv_done, B * CPB)
                pool.tensor_copy(x2_hi[:, tiles, :], x2[:, tiles, :]).then_inc(x2_hi_done, 1)
                pool.wait_ge(x2_hi_done, j + 1)
                pool.tensor_tensor(x2_lo[:, tiles, :], x2[:, tiles, :], x2_hi[:, tiles, :].bitcast(F32),
                                   ALU.subtract).then_inc(x2_lo_done, 1)

        @block.sync
        def _(sp):
            sp.dma_start(emb_sb[0:VOCAB, :], emb).then_inc(tables_loaded, 16)
            sp.dma_start(conv_sb[0:VOCAB, :, :].rearrange("p k d -> p (k d)"),
                         conv.rearrange("(o k) d -> o (k d)", o=1).partition_broadcast(VOCAB)
                         ).then_inc(tables_loaded, 16)
            for b in range(B):
                sp.dma_start(tok_sb[b], tok[b:b + 1, :].partition_broadcast(VOCAB)).then_inc(tok_loaded, 16)

            def weights(index):
                sp.dma_start(w_slot[:, :, :].rearrange("p w c -> p (w c)"), w_pairs[index, :, :]
                             ).then_inc(w_loaded, 16)

            def head_qk(k):
                rows = slice(DH * k, DH * (k + 1))
                for part in range(2):
                    half = slice(DH * part, DH * (part + 1))
                    for dst, w, low in ((q_st, 0, part), (k_hi, 1, 0), (k_lo, 1, 1)):
                        sp.dma_start(dst[half, k, :].bitcast(F32), pair_qk[rows, w, low, :]
                                     ).then_inc(qk_loaded[k], 16)

            def head_v(h, k):
                sp.dma_start(v_slot[:, k, :, :].bitcast(F32), v_all[:, :, h, :].bitcast(F32)
                             ).then_inc(vs_loaded[k], 16)

            sp.dma_start(wo_sb[:, :, :], wo_dup).then_inc(wout_loaded, 16)
            sp.dma_start(uo_sb[:, :], u_out).then_inc(wout_loaded, 16)
            sp.dma_start(wor_sb, wo_rows).then_inc(wout_loaded, 16)
            weights(0)
            sp.dma_start(wv_sb[:, :], wv).then_inc(attn_loaded, 16)
            sp.dma_start(b_sb[:, :], b_out.partition_broadcast(P)).then_inc(attn_loaded, 16)
            sp.dma_start(ctrl_sb[:, :], controller).then_inc(ffn_loaded, 16)
            sp.dma_start(f1_sb[:, :], f1).then_inc(ffn_loaded, 16)
            sp.dma_start(f2_sb[:, :, :], f2).then_inc(ffn_loaded, 16)
            sp.wait_ge(work_mm, 4)
            weights(1)
            sp.wait_ge(work_read, 4)
            head_qk(0)
            sp.wait_ge(v_lo_done, NT)
            head_v(0, 0)

            def pair_loads(pair):
                if pair.i > 0:
                    wait_apart(sp, scores_ready, pair.step0)
                head_qk(1)
                if pair.i == 4:
                    wait_apart(sp, work_read, pair.use_of("v7"))
                    wait_apart(sp, pv_done, pair.chunk0 - CPH)
                    head_v(0, 0)
                if pair.i > 0:
                    wait_apart(sp, pv_done, pair.chunk0)
                head_v(pair.head + 1, 1)
                if pair.i < 7:
                    wait_apart(sp, work_mm, pair.use_of("k1"))
                    weights(pair.head_pair + 2)
                    wait_apart(sp, work_read, pair.use_of("k1"))
                    wait_apart(sp, scores_ready, pair.step0 + SPH)
                    head_qk(0)
                    if pair.i != 3:
                        wait_apart(sp, pv_done, pair.chunk0 + CPH)
                        head_v(pair.head + 2, 0)

            run_pairs(sp, pair_loads)

            for t in range(TILES):
                sp.wait_ge(result_done, t + 1)
                sp.dma_start(out[t * P:(t + 1) * P, :], result[:, t, :]).then_inc(stored, 16)
            sp.wait_ge(stored, 16 * TILES)

        @block.tensor
        def _(pe):
            def embed(c):
                b = c // 2
                for t in range(4 * (c % 2), 4 * (c % 2) + 4):
                    dst = ps[:, c, (t % 4) * P:(t % 4 + 1) * P]
                    pe.matmul(dst, one_hot[b][:, t * P:(t + 1) * P], table[0:VOCAB, 0, :], start=True, stop=False)
                    ins = pe.matmul(dst, one_hot[b][:, 1 + t * P:1 + (t + 1) * P], table[0:VOCAB, 1, :],
                                    start=False, stop=True)
                ins.then_inc(h_mm, 1)

            pe.wait_ge(wqkv_loaded, 32)
            for t in range(12):
                last = pe.matmul(ps[:, 4, t:t + 1], wt_sb[:, t * P:(t + 1) * P], u_sb[:, :],
                                 start=True, stop=True)
            last.then_inc(setup_pe, 1)
            pe.wait_ge(wout_loaded, 16 * 6)
            for h in range(H):
                last = pe.matmul(ps[:, 5, 0:1], wo_sb[0:DH, h, :], uo_sb[:, h:h + 1],
                                 start=h == 0, stop=h == H - 1)
            last.then_inc(setup_pe, 1)
            pe.wait_ge(setup_dve, SETUP_TABLES)
            pe.wait_ge(one_hot_ready, 2 * B)
            embed(0)
            embed(1)
            pe.wait_ge(wqkv_rows_loaded, 16)
            pe.wait_ge(setup_act, 2)
            for t in range(12):
                last = pe.matmul(ps[:, 6, 0:1], wr_sb[:, t, :], norm_sb[:, t:t + 1],
                                 start=t == 0, stop=t == 11)
            last.then_inc(setup_pe, 1)
            pe.wait_ge(setup_act, 3)
            for t in range(4):
                last = pe.matmul(ps[:, 7, t:t + 1], wor_sb[:, t * P:(t + 1) * P], norm_sb[:, 12:13],
                                 start=True, stop=True)
            last.then_inc(setup_pe, 1)
            embed(2)
            pe.wait_ge(setup_dve, SETUP_SQUARES)
            pe.wait_ge(const_ready, N_CONST)
            pe.matmul(ps[:, 4, 0:4], ones[:, :], norm_sb[:, 18:22], start=True, stop=True).then_inc(setup_pe, 1)
            embed(3)
            for t in range(NT):
                pe.wait_ge(xhat_done, t + 1)
                ins = pe.transpose(ps[:, 5 + t // 4, (t % 4) * P:(t % 4 + 1) * P], x_hat[0][:, t, :], ident[:, :])
                if t % 4 == 3:
                    ins.then_inc(xt_mm, 1)

            def project_values(t, bank):
                return pe.matmul(ps[:, bank, :], xt[:, t * P:(t + 1) * P], wv_sb[:, :], start=True, stop=True)

            def project_qk(kind, bank=WORK):
                which, c = "qk".index(kind[0]), int(kind[1])
                return pe.matmul(ps[:, bank, :], w_slot[:, which, :], xt[:, c * HALF:(c + 1) * HALF],
                                 start=True, stop=True)

            pe.wait_ge(h_ready, 4)
            pe.wait_ge(w_loaded, 16)
            pe.wait_ge(xt_done, 2)
            for kind in SETUP_QK:
                project_qk(kind, SETUP_QK[kind]).then_inc(work_mm, 1)
            pe.wait_ge(attn_loaded, 32)
            pe.wait_ge(setup_dve, SETUP_RATIO)
            for t in range(NT):
                if t >= 2:
                    pe.wait_ge(v_lo_done, t - 1)
                project_values(t, 3 + t % 2).then_inc(v_mm, 1)
            pe.wait_ge(v_lo_done, NT)

            def scores(pair, k, t):
                n = pair.step0 + k * SPH + t
                if t == 0:
                    pe.wait_ge(qk_loaded[k], 6 * pair.slot_loads)
                if not (pair.i == 0 and k == 0 and t < 2):
                    pe.wait_ge(exp_done, n - 1)
                for c in range(2):
                    bank = ps[:, SCORES + 2 * (t % 2) + c, :]
                    q = q_st[:, k, t * P:(t + 1) * P]
                    half = slice(c * HALF, (c + 1) * HALF)
                    pe.matmul(bank, q, k_hi[:, k, half], start=True, stop=False)
                    if c == t // 4:
                        pe.matmul(bank[:, (t % 4) * P:(t % 4 + 1) * P], neg_diag[:, :], ident_b[:, :],
                                  start=False, stop=False)
                    ins = pe.matmul(bank, q, k_lo[:, k, half], start=False, stop=True)
                ins.then_inc(scores_ready, 1)

            def transposes(n, t, a, begins):
                m = n - T_LAG
                if a == 0:
                    pe.wait_ge(norm_done, m + 1)
                if not begins:
                    pe.wait_ge(lo_done, 2 * m - 1 + a)
                for q in range(4):
                    col = (4 * a + q) * P
                    ins = pe.transpose(ps[:, TRANS + a, q * P:(q + 1) * P],
                                       probs[:, (t - T_LAG) % 4, col:col + P], ident[:, :])
                ins.then_inc(pt_ready, 1)

            def values(chunk, c_local, slot, slot_loads, quarter, begins):
                if quarter == 0:
                    pe.wait_ge(lo_done, 4 * chunk + 4)
                    if not begins:
                        pe.wait_ge(o_done, chunk)
                    if c_local == 0:
                        pe.wait_ge(vs_loaded[slot], slot_loads)
                for jt in (2 * quarter, 2 * quarter + 1):
                    for src in (pt_hi, pt_lo):
                        ins = pe.matmul(ps[:, PV_BANK, 0:CW], v_slot[:, slot, jt, :], src[:, c_local % 2, jt, :],
                                        start=jt == 0 and src is pt_hi, stop=jt == NT - 1 and src is pt_lo)
                if quarter == 3:
                    ins.then_inc(pv_done, 1)

            def lagging(pair, k, t, drain=False):
                n = pair.step0 + k * SPH + t
                fresh = pair.i == 0 and k == 0
                tr = not (fresh and t < T_LAG) and not (drain and t >= T_LAG)
                late = t - PV_LAG - (t % 2 == 0)
                pv = not (fresh and late < 0) and not (drain and late >= 0)
                c_local = late // 2 % CPH
                chunk = pair.chunk0 + k * CPH + late // 2
                slot = k if late >= 0 else 1 - k
                loads = pair.slot_loads - (16 if k == 0 and late < 0 else 0)
                for half in range(2):
                    if tr:
                        transposes(n, t, half, fresh and t == T_LAG)
                    if half == 1:
                        work(pair, k, t)
                    if pv:
                        values(chunk, c_local, slot, loads, half + (2 if t % 2 == 0 else 0),
                               fresh and t == PV_LAG)

            def work(pair, k, t):
                kind = pair.work.get((k, t))
                if not kind:
                    return
                pe.wait_ge(work_read, pair.use(k, t) - 1)
                if kind == "q0":
                    pe.wait_ge(w_loaded, 16 * (pair.index + 2))
                if kind in ("q0", "q1") and pair.i == 3:
                    pe.wait_ge(xt_done, 2 + int(kind[1]) + 1)
                if kind[0] in "qk":
                    ins = project_qk(kind)
                elif kind[0] == "v":
                    ins = project_values(int(kind[1]), WORK)
                elif kind[0] == "x":
                    pe.wait_ge(xhat_done, 2 * NT)
                    for j in range(4):
                        ins = pe.transpose(ps[:, WORK, j * P:(j + 1) * P], x_hat[1][:, 4 * int(kind[1]) + j, :],
                                           ident[:, :])
                else:
                    pe.wait_ge(o_done, pair.chunk0 + k * CPH - (2 if kind == "y0" else 0))
                    head = pair.head + k - 1 if not (pair.i % 4 == 0 and k == 0) else H - 1
                    for j in range(4):
                        tile = 4 * int(kind[1]) + j
                        ins = pe.matmul(ps[:, WORK, j * P:(j + 1) * P], o_slot[:, 1 - k, tile * P:(tile + 1) * P],
                                        wo_sb[:, head, :], start=True, stop=True)
                ins.then_inc(work_mm, 1)

            def pair_steps(pair):
                for k in range(2):
                    for t in range(SPH):
                        scores(pair, k, t)
                        lagging(pair, k, t)

            run_pairs(pe, pair_steps)
            drain = Pair(8)
            for t in range(SPH):
                lagging(drain, 0, t, drain=True)

            for t in range(TILES):
                pe.wait_ge(x2_done, t + 1)
                ins = pe.transpose(ps[:, t // 4, (t % 4) * P:(t % 4 + 1) * P], x2[:, t, :], ident[:, :])
                if t % 4 == 3:
                    ins.then_inc(x2t_mm, 1)

            pe.wait_ge(ffn_loaded, 48)
            pe.wait_ge(x2t_done, 4)
            x2_pairs = x2t[:, :].rearrange("p (j u t) -> p j u t", u=2, t=GROUP)
            for c in range(2):
                for u in range(2):
                    ins = pe.matmul(ps[u * ES:(u + 1) * ES, 6 + c, :], ctrl_sb[:, :],
                                    x2_pairs[:, c * PAIRS // 2:(c + 1) * PAIRS // 2, u, :], start=True, stop=True)
            ins.then_inc(logit_mm, 1)
            pe.wait_ge(choose, 4)
            perm_flat = x2t[:, :]

            def perm_t(i):
                if i >= 2:
                    pe.wait_ge(spread_done, i - 1)
                pe.transpose(ps[:, 4 + i % 2, 0:P], perm_flat[:, i * P:(i + 1) * P], ident[:, :]).then_inc(permt_mm, 1)

            perm_t(0)
            for i in range(TILES):
                if i + 1 < TILES:
                    perm_t(i + 1)
                if i % 4 == 0:
                    pe.wait_ge(x2_lo_done, i // 4 + 1)
                pe.wait_ge(spread_done, i + 1)
                if i >= 2:
                    pe.wait_ge(taken_done, i - 1)
                mov = spread[:, i % 2, :, :]
                pe.matmul(ps[:, 2 + i % 2, :], x2_hi[:, i, :], mov, start=True, stop=False)
                pe.matmul(ps[:, 2 + i % 2, :], x2_lo[:, i, :], mov, start=False, stop=True).then_inc(taken_mm, 1)
            pe.wait_ge(taken_done, TILES)
            for k in range(NK):
                for q in range(4):
                    e = 4 * k + q
                    ins = pe.matmul(ps[32 * q:32 * (q + 1), k // 4, (k % 4) * GROUPS:(k % 4 + 1) * GROUPS],
                                    f1_sb[:, e * F:(e + 1) * F], taken[:, e, :], start=True, stop=True,
                                    tile_position=(0, 32 * q))
                if k % 4 == 3:
                    ins.then_inc(hid_mm, 1)
            for k in range(NK):
                pe.wait_ge(hid_done, k + 1)
                if k >= 2:
                    pe.wait_ge(int_done, k - 1)
                pe.matmul(ps[:, 4 + k % 2, :], f2_sb[:, k, :], hidden[:, k % 2, :],
                          start=True, stop=True).then_inc(int_mm, 1)
            pe.wait_ge(int_done, NK)

            def pair_transposes(i):
                if i >= 2:
                    pe.wait_ge(intp_done, i - 1)
                for j in range(PPT):
                    ins = pe.transpose(ps[:, 6 + i % 2, j * P:(j + 1) * P], inter_t[:, PPT * i + j, :], ident[:, :])
                ins.then_inc(intp_mm, 1)

            pair_transposes(0)
            for i in range(TILES):
                if i + 1 < TILES:
                    pair_transposes(i + 1)
                pe.wait_ge(intp_done, i + 1)
                if i >= 4:
                    pe.wait_ge(result_done, i - 3)
                for j in range(PPT):
                    ins = pe.matmul(ps[32 * j:32 * (j + 1), i % 4, 0:D], perm[:, PPT * i + j, :],
                                    inter_p[:, PPT * i + j, :], start=True, stop=True, tile_position=(0, 32 * j))
                ins.then_inc(res_mm, 1)

        @block.scalar
        def _(act):
            act.dma_start(wt_sb, wqkv_t).then_inc(wqkv_loaded, 16)
            act.dma_start(u_sb[:, :], u_qkv).then_inc(wqkv_loaded, 16)
            act.dma_start(wr_sb, wqkv_rows).then_inc(wqkv_rows_loaded, 16)
            for i, x in enumerate((sigma_qkv, sigma_out, temperature)):
                act.dma_start(sig[:, i:i + 1], x.partition_broadcast(P)).then_inc(wout_loaded, 16)

            def embedded(b):
                for c in (2 * b, 2 * b + 1):
                    act.wait_ge(h_mm, c + 1)
                    act.activation(h_sb[:, 4 * c:4 * c + 4, :], ps[:, c, :].rearrange("p (t d) -> p t d", d=D),
                                   ACT.Relu).then_inc(h_ready, 1)

            act.wait_ge(wout_loaded, 16 * 6)
            act.activation(norm_sb[:, 28:29], sig[:, 2:3], ACT.Exp).then_inc(setup_act, 1)
            act.wait_ge(setup_pe, 1)
            act.activation(norm_sb[:, 0:12], ps[:, 4, 0:12], ACT.Copy).then_inc(setup_act, 1)
            act.wait_ge(setup_pe, 2)
            act.activation(norm_sb[:, 12:13], ps[:, 5, 0:1], ACT.Copy).then_inc(setup_act, 1)
            embedded(0)
            act.wait_ge(setup_pe, 3)
            act.activation(norm_sb[:, 13:14], ps[:, 6, 0:1], ACT.Copy).then_inc(setup_act, 1)
            act.wait_ge(setup_pe, 4)
            act.activation(norm_sb[:, 14:18], ps[:, 7, 0:4], ACT.Copy).then_inc(setup_act, 1)
            embedded(1)
            for c in range(2):
                act.wait_ge(xt_mm, c + 1)
                act.activation(xt[:, c * HALF:(c + 1) * HALF], ps[:, 5 + c, :], ACT.Copy).then_inc(xt_done, 1)

            q_scale, v_scale = norm_sb[:, 31:32], norm_sb[:, 29:30]
            act.wait_ge(setup_dve, SETUP_SCALES)

            def high_qk(kind, bank=WORK):
                which, c = "qk".index(kind[0]), int(kind[1])
                dst = pair_qk[:, which, 0, c * HALF:(c + 1) * HALF].bitcast(F32R)
                if which == 0:
                    return act.activation(dst, ps[:, bank, :], ACT.Copy, scale=q_scale)
                return act.activation(dst, ps[:, bank, :], ACT.Copy)

            def high_values(t, bank):
                return act.activation(v_all[:, t, :, 0:DH], ps[:, bank, :].rearrange("p (h c) -> p h c", c=DH),
                                      ACT.Copy, scale=v_scale)

            for j, kind in enumerate(SETUP_QK):
                act.wait_ge(work_mm, j + 1)
                high_qk(kind, SETUP_QK[kind]).then_inc(work_hi, 1)
            for t in range(NT):
                act.wait_ge(v_mm, t + 1)
                high_values(t, 3 + t % 2).then_inc(v_hi_done, 1)

            def work(pair, k, t):
                kind = pair.work.get((k, t))
                if not kind or kind[0] == "y":
                    return
                act.wait_ge(work_mm, pair.use(k, t))
                if kind[0] in "qk":
                    if kind == "q0":
                        act.wait_ge(qk_loaded[1], 6 * pair.slot_loads)
                    high_qk(kind).then_inc(work_hi, 1)
                elif kind[0] == "v":
                    if kind == "v0":
                        act.wait_ge(vs_loaded[1], pair.slot_loads)
                    high_values(int(kind[1]), WORK).then_inc(work_hi, 1)
                else:
                    c = int(kind[1])
                    act.activation(xt[:, c * HALF:(c + 1) * HALF], ps[:, WORK, :], ACT.Copy
                                   ).then_inc(xt_done, 1)
                    act.wait_ge(xt_done, 2 + c + 1)
                    act.sem_inc(work_read, 1)

            def lagging(pair, k, t, drain=False):
                n = pair.step0 + k * SPH + t
                fresh = pair.i == 0 and k == 0
                if t % 2 and not (fresh and t < PV_LAG + 2):
                    c_local = (t - PV_LAG - 2) // 2
                    if not (drain and c_local >= 0):
                        slot = k if c_local >= 0 else 1 - k
                        cols = slice((c_local % CPH) * CW, (c_local % CPH + 1) * CW)
                        act.wait_ge(pv_done, pair.chunk0 + k * CPH + c_local + 1)
                        act.activation(o_slot[:, slot, cols], ps[:, PV_BANK, 0:CW], ACT.Copy).then_inc(o_done, 1)
                idle = (fresh and t < T_LAG) or (drain and t >= T_LAG)
                m_local = (t - T_LAG) % SPH
                for a in range(2):
                    if idle:
                        break
                    act.wait_ge(pt_ready, 2 * (n - T_LAG) + a + 1)
                    if a == 0 and not (fresh and t - T_LAG < 4):
                        act.wait_ge(pv_done, pair.chunk0 + k * CPH + (t - T_LAG) // 2 - 1)
                    dst = pt_hi[:, m_local // 2 % 2, 4 * a:4 * a + 4, (m_local % 2) * P:(m_local % 2 + 1) * P]
                    act.activation(dst, ps[:, TRANS + a, :].rearrange("p (j c) -> p j c", c=P),
                                   ACT.Copy).then_inc(hi_done, 1)

            def exponentials(pair, k, t):
                n = pair.step0 + k * SPH + t
                act.wait_ge(max_done, n + 1)
                if not (pair.i == 0 and k == 0 and t < 4):
                    act.wait_ge(pt_ready, 2 * n - 6)
                act.activation(probs[:, t % 4, :].rearrange("p (a c) -> p a c", a=2),
                               ps[:, SCORES + 2 * (t % 2):SCORES + 2 * (t % 2) + 2, :], ACT.Exp,
                               bias=neg_max[:, t % 4:t % 4 + 1],
                               accum_out=row_sum[:, t % 4:t % 4 + 1]).then_inc(exp_done, 1)

            def pair_steps(pair):
                for k in range(2):
                    for t in range(SPH):
                        lagging(pair, k, t)
                        work(pair, k, t)
                        exponentials(pair, k, t)

            run_pairs(act, pair_steps)
            for t in range(PV_LAG + 1):
                lagging(Pair(8), 0, t, drain=True)

            for c in range(4):
                act.wait_ge(x2t_mm, c + 1)
                act.activation(x2t[:, c * HALF:(c + 1) * HALF], ps[:, c, :], ACT.Copy).then_inc(x2t_done, 1)

            for i in range(TILES):
                act.wait_ge(taken_mm, i + 1)
                act.activation(taken[:, :, 8 * i:8 * i + 8].rearrange("p e g -> p g e"),
                               ps[:, 2 + i % 2, :].rearrange("p (g e) -> p g e", e=ES),
                               ACT.Copy).then_inc(taken_done, 1)
            act.wait_ge(hid_mm, 4)
            inter_v = inter_t.rearrange("p j (u e) -> p e j u", u=2)
            for k in range(NK):
                act.wait_ge(int_mm, k + 1)
                act.activation(inter_v[:, 4 * k:4 * k + 4, :, :],
                               ps[:, 4 + k % 2, :].rearrange("p (q j u) -> p q j u", q=4, u=2),
                               ACT.Copy).then_inc(int_done, 1)
            for i in range(TILES):
                act.wait_ge(intp_mm, i + 1)
                act.activation(inter_p[:, PPT * i:PPT * (i + 1), :],
                               ps[:, 6 + i % 2, :].rearrange("p (j d) -> p j d", d=D), ACT.Copy).then_inc(intp_done, 1)

        @block.vector
        def _(dve):
            count = [0]

            def link(ins):
                count[0] += 1
                ins.then_inc(setup_dve, 1)
                dve.wait_ge(setup_dve, count[0])

            for b in range(B):
                dve.wait_ge(tok_loaded, 16 * B)
                dve.wait_ge(const_ready, N_CONST)
                dve.memset(one_hot[b][:, 0:1], 0.0).then_inc(one_hot_ready, 1)
                dve.tensor_scalar(one_hot[b][:, 1:SEQ + 1], tok_sb[b], float(VOCAB - 1), vocab_id[0:VOCAB, :],
                                  ALU.min, ALU.is_equal).then_inc(one_hot_ready, 1)
            link(dve.memset(qs[:, :], 0.0))
            dve.wait_ge(tables_loaded, 32)
            link(dve.tensor_reduce(qs[0:VOCAB, 0:1], emb_sb[0:VOCAB, :], AXX, ALU.max, apply_absolute_value=True))
            link(dve.tensor_reduce(qs[0:VOCAB, 2:3], conv_sb[0:VOCAB, :, :].rearrange("p k d -> p (k d)"), AXX,
                                   ALU.max, apply_absolute_value=True))
            dve.wait_ge(setup_pool, 1)
            link(dve.tensor_scalar(qs[0:VOCAB, 3:5], qs[0:VOCAB, 1:3], 1.0 / QMAX, None, ALU.mult))
            link(dve.reciprocal(qs[0:VOCAB, 5:7], qs[0:VOCAB, 3:5]))
            parts = [(emb_sb[0:VOCAB, :], quant[0:VOCAB, 0:D], 0),
                     (conv_sb[0:VOCAB, :, :].rearrange("p k d -> p (k d)"), quant[0:VOCAB, D:3 * D], 1)]
            for w, q, i in parts:
                link(dve.tensor_scalar(q, w, qs[0:VOCAB, 5 + i:6 + i], ROUND, ALU.mult, ALU.add))
                link(dve.tensor_scalar(q, q, ROUND, qs[0:VOCAB, 3 + i:4 + i], ALU.subtract, ALU.mult))
                link(dve.tensor_tensor(q, q, w, ALU.subtract))
                link(dve.tensor_tensor(q, w, q, ALU.add))
            for k in range(2):
                link(dve.tensor_tensor(table[0:VOCAB, k, :], quant[0:VOCAB, 0:D],
                                       quant[0:VOCAB, D * (k + 1):D * (k + 2)], ALU.mult))
            assert count[0] == SETUP_TABLES

            def tile_statistics(t):
                dve.bn_stats(stats[:, t, :], h_sb[:, t, :]).then_inc(stat_done, 1)

            def variances(b, first):
                done = (0 if first else TILES) + (b + 1) * NT
                for t in range(b * NT, (b + 1) * NT):
                    dve.wait_ge(stat_done, done - NT + t % NT + 1)
                    ins = dve.bn_aggr(mv[:, t, :], stats[:, t, :])
                ins.then_inc(setup_norm, 1)
                dve.wait_ge(setup_norm, b + 1 if first else B + b + 1)
                tiles = slice(b * NT, (b + 1) * NT)
                dve.tensor_scalar(rstd[:, tiles], mv[:, tiles, 1], EPS, None, ALU.add).then_inc(aggr_done, 1)

            def normalise_tile(t, dst, done):
                dve.tensor_scalar(dst, h_sb[:, t, :], mv[:, t, 0:1], rstd[:, t:t + 1],
                                  ALU.subtract, ALU.mult).then_inc(done, 1)

            for t in range(NT):
                if t % 4 == 0:
                    dve.wait_ge(h_ready, t // 4 + 1)
                tile_statistics(t)
            variances(0, True)
            dve.wait_ge(setup_act, 5)
            sq = norm_sb[:, 22:24]
            scratch = quant[:, 0:12]
            for a, n, col in ((0, 12, 18), (12, 1, 19), (13, 1, 20), (14, 4, 21)):
                v = norm_sb[:, a:a + n]
                link(dve.tensor_tensor(scratch[:, 0:n], v, v, ALU.mult))
                link(dve.tensor_reduce(norm_sb[:, col:col + 1], scratch[:, 0:n], AXX, ALU.add))
            assert count[0] == SETUP_SQUARES
            dve.wait_ge(rstd_done, 1)
            for t in range(NT):
                normalise_tile(t, x_hat[0][:, t, :], xhat_done)
            dve.wait_ge(setup_pe, 5)
            link(dve.reciprocal(sq, ps[:, 4, 2:4]))
            link(dve.tensor_tensor(norm_sb[:, 24:26], ps[:, 4, 0:2], sq, ALU.mult))
            assert count[0] == SETUP_RATIO
            dve.wait_ge(setup_pool, 2)
            dve.wait_ge(wout_loaded, 16 * 6)
            dve.wait_ge(setup_act, 5)
            link(dve.tensor_tensor(norm_sb[:, 29:31], norm_sb[:, 26:28], sig[:, 0:2], ALU.mult))
            link(dve.scalar_tensor_tensor(norm_sb[:, 31:32], norm_sb[:, 29:30], norm_sb[:, 28:29],
                                          norm_sb[:, 29:30], ALU.mult, ALU.mult))
            assert count[0] == SETUP_SCALES
            q_scale, v_scale, o_scale = norm_sb[:, 31:32], norm_sb[:, 29:30], norm_sb[:, 30:31]
            dve.wait_ge(const_ready, N_CONST)

            def low_qk(kind, bank=WORK):
                which, c = "qk".index(kind[0]), int(kind[1])
                high = pair_qk[:, which, 0, c * HALF:(c + 1) * HALF]
                dst = pair_qk[:, which, 1, c * HALF:(c + 1) * HALF].bitcast(F32R)
                if which == 0:
                    return dve.scalar_tensor_tensor(dst, ps[:, bank, :], q_scale, high, ALU.mult, ALU.subtract)
                return dve.tensor_tensor(dst, ps[:, bank, :], high, ALU.subtract)

            def low_values(t, bank):
                return dve.scalar_tensor_tensor(
                    v_all[:, t, :, DH:P], ps[:, bank, :].rearrange("p (h c) -> p h c", c=DH), v_scale,
                    v_all[:, t, :, 0:DH].bitcast(F32), ALU.mult, ALU.subtract)

            for j, kind in enumerate(SETUP_QK):
                dve.wait_ge(work_hi, j + 1)
                low_qk(kind, SETUP_QK[kind]).then_inc(work_read, 1)
            for t in range(NT):
                dve.wait_ge(v_hi_done, t + 1)
                low_values(t, 3 + t % 2).then_inc(v_lo_done, 1)

            def spread_norm(b, first, k, t):
                if k == 0:
                    if t == 0 and first:
                        dve.wait_ge(h_ready, 4)
                    tile_statistics(b * NT + t)
                elif t == 0:
                    variances(b, first)
                elif 3 <= t < 7:
                    if t == 3:
                        dve.wait_ge(rstd_done, b + 1 if first else B + b + 1)
                    for i in (2 * (t - 3), 2 * (t - 3) + 1):
                        if first:
                            normalise_tile(b * NT + i, x_hat[1][:, i, :], xhat_done)
                        else:
                            normalise_tile(b * NT + i, x2[:, b * NT + i, :], x2_done)

            def work(pair, k, t):
                kind = pair.work.get((k, t))
                if not kind or kind[0] == "x":
                    return
                if kind[0] == "y":
                    if pair.i in (0, 4) and kind == "y0":
                        dve.wait_ge(bias_added, 1 if pair.i == 0 else B)
                    dve.wait_ge(work_mm, pair.use(k, t))
                    first = (pair.i - (k == 0)) // 4 * NT + 4 * int(kind[1])
                    tiles = slice(first, first + 4)
                    dve.scalar_tensor_tensor(h_sb[:, tiles, :], ps[:, WORK, :].rearrange("p (t d) -> p t d", d=D),
                                             o_scale, h_sb[:, tiles, :], ALU.mult, ALU.add).then_inc(work_read, 1)
                    return
                dve.wait_ge(work_hi, pair.high(k, t))
                if kind[0] == "v":
                    low_values(int(kind[1]), WORK).then_inc(work_read, 1)
                else:
                    low_qk(kind).then_inc(work_read, 1)

            def lagging(pair, k, t, drain=False):
                n = pair.step0 + k * SPH + t
                fresh = pair.i == 0 and k == 0
                if (fresh and t < T_LAG) or (drain and t >= T_LAG):
                    return
                m_local = (t - T_LAG) % SPH
                for a in range(2):
                    at = (slice(None), m_local // 2 % 2, slice(4 * a, 4 * a + 4),
                          slice((m_local % 2) * P, (m_local % 2 + 1) * P))
                    dve.wait_ge(hi_done, 2 * (n - T_LAG) + a + 1)
                    dve.tensor_tensor(pt_lo[at], ps[:, TRANS + a, :].rearrange("p (j c) -> p j c", c=P),
                                      pt_hi[at].bitcast(F32), ALU.subtract).then_inc(lo_done, 1)

            def reciprocals(pair, k, t):
                n = pair.step0 + k * SPH + t
                dve.wait_ge(exp_done, n)
                dve.reciprocal(inv_sum[:, (t - 1) % 4:(t - 1) % 4 + 1],
                               row_sum[:, (t - 1) % 4:(t - 1) % 4 + 1]).then_inc(recip_done, 1)

            def maxima(pair, k, t):
                n = pair.step0 + k * SPH + t
                dve.wait_ge(scores_ready, n + 1)
                dve.tensor_reduce(neg_max[:, t % 4:t % 4 + 1],
                                  ps[:, SCORES + 2 * (t % 2):SCORES + 2 * (t % 2) + 2, :].rearrange(
                                      "p a c -> p (a c)"), AXX, ALU.max, negate=True).then_inc(max_done, 1)

            def pair_steps(pair):
                for k in range(2):
                    for t in range(SPH):
                        maxima(pair, k, t)
                        if not (pair.i == 0 and k == 0 and t == 0):
                            reciprocals(pair, k, t)
                        lagging(pair, k, t)
                        work(pair, k, t)
                        if pair.i == 0:
                            spread_norm(1, True, k, t)
                        elif pair.i == 7:
                            if k == 0 and t == 0:
                                dve.wait_ge(work_read, pair.uses)
                            spread_norm(0, False, k, t)

            run_pairs(dve, pair_steps)
            drain = Pair(8)
            reciprocals(drain, 0, 0)
            for t in range(SPH):
                lagging(drain, 0, t, drain=True)
                work(drain, 0, t)
            dve.wait_ge(work_read, drain.uses + 2)
            for t in range(NT, TILES):
                tile_statistics(t)
            variances(1, False)
            dve.wait_ge(rstd_done, 2 * B)
            for t in range(NT, TILES):
                normalise_tile(t, x2[:, t, :], x2_done)

            dve.wait_ge(logit_mm, 1)
            lg = logits.rearrange("p (j t) -> p j t", t=GROUP)
            dve.tensor_tensor(lg, ps[:, 6:8, :].rearrange("p c (j t) -> p (c j) t", t=GROUP),
                              tie[:, :].unsqueeze(1).broadcast_to([P, PAIRS, GROUP]), ALU.add).then_inc(choose, 1)
            dve.wait_ge(choose, 1)
            dve.tensor_reduce(group_max[:, :], lg, AXX, ALU.max).then_inc(choose, 1)
            dve.wait_ge(choose, 2)
            dve.wait_ge(perm_zero, 1)
            for u in range(2):
                rows = slice(u * ES, (u + 1) * ES)
                dve.tensor_tensor(perm[rows, :, u * GROUP:(u + 1) * GROUP], lg[rows, :, :],
                                  group_max[rows, :].unsqueeze(2).broadcast_to([ES, PAIRS, GROUP]),
                                  ALU.is_equal).then_inc(choose, 1)
            for i in range(TILES):
                dve.wait_ge(permt_mm, i + 1)
                if i >= 2:
                    dve.wait_ge(taken_mm, i - 1)
                dve.tensor_tensor(spread[:, i % 2, :, :],
                                  ps[:, 4 + i % 2, 0:P].unsqueeze(1).broadcast_to([P, 4, P]),
                                  quad[:, :].unsqueeze(2).broadcast_to([P, 4, P]), ALU.mult).then_inc(spread_done, 1)
            for k in range(NK):
                dve.wait_ge(hid_mm, k // 4 + 1)
                if k >= 2:
                    dve.wait_ge(int_mm, k - 1)
                dve.scalar_tensor_tensor(
                    hidden[:, k % 2, :].rearrange("p (q g) -> p q g", q=4),
                    ps[:, k // 4, (k % 4) * GROUPS:(k % 4 + 1) * GROUPS].unsqueeze(1).broadcast_to([P, 4, GROUPS]),
                    0.0, quad[:, :].unsqueeze(2).broadcast_to([P, 4, GROUPS]), ALU.max,
                    ALU.mult).then_inc(hid_done, 1)
            for i in range(TILES):
                dve.wait_ge(res_mm, i + 1)
                dve.tensor_tensor(result[:, i, :], ps[:, i % 4, 0:D], h_sb[:, i, :], ALU.add).then_inc(result_done, 1)


SETUP_TABLES = 15
SETUP_SQUARES = SETUP_TABLES + 8
SETUP_RATIO = SETUP_SQUARES + 2
SETUP_SCALES = SETUP_RATIO + 2


def kernel(**inputs):
    import concourse.bacc as bacc
    from concourse.bass_utils import run_bass_kernel_spmd

    a = {k: np.asarray(v) for k, v in inputs.items()}
    w = a["L0_attn_w_qkv"]
    wo = a["L0_attn_w_out"]

    pairs = w[:2 * H * DH].reshape(2, H // 2, P, D).transpose(1, 3, 0, 2).reshape(H // 2, D, 2 * P)
    wo_t = wo.reshape(D, H, DH).transpose(2, 1, 0)
    arrays = {
        "tok": a["x"].astype(np.int32, copy=False),
        "emb": a["L0_tok_emb_weight"],
        "conv": a["L0_tok_conv_weight"].reshape(D, 2).T,
        "w_pairs": np.concatenate([pairs, pairs[:2]], axis=0),
        "wv": w[2 * H * DH:].T,
        "wqkv_t": w.T,
        "wqkv_rows": w.reshape(12, P, D).transpose(1, 0, 2),
        "u_qkv": a["L0_attn_u_qkv"].reshape(D, 1),
        "wo_dup": np.concatenate([wo_t, wo_t], axis=0),
        "wo_rows": wo,
        "u_out": a["L0_attn_u_out"].reshape(H, DH).T,
        "sigma_qkv": a["L0_attn_sigma_qkv"].reshape(1, 1),
        "sigma_out": a["L0_attn_sigma_out"].reshape(1, 1),
        "temperature": a["L0_attn_temperature"].reshape(1, 1),
        "b_out": a["L0_attn_b_out"].reshape(1, D),
        "controller": a["L0_ffn_controller"].reshape(D, ES),
        "f1": a["L0_ffn_f1"].reshape(D, ES * F),
        "f2": a["L0_ffn_f2"].reshape(NK, P, D).transpose(1, 0, 2),
    }
    nc = bacc.Bacc("TRN2", target_bir_lowering=False, num_devices=1)
    feeds, args = {}, []
    for name, x in arrays.items():
        x = np.ascontiguousarray(x)
        feeds["in_" + name] = x
        args.append(nc.dram_tensor("in_" + name, x.shape, mybir.dt.from_np(x.dtype), kind="ExternalInput").ap())
    args.append(nc.dram_tensor("out_h", (B * SEQ, D), F32, kind="ExternalOutput").ap())
    layer_kernel(nc, *args)
    r = run_bass_kernel_spmd(nc, [feeds], core_ids=[0])
    return r.results[0]["out_h"].reshape(B, SEQ, D)
```

```python
import numpy as np
from contextlib import ExitStack

import concourse.bass as bass
from concourse import mybir

F32 = mybir.dt.float32
F32R = mybir.dt.float32r
BF16 = mybir.dt.bfloat16
I32 = mybir.dt.int32
ALU = mybir.AluOpType
ACT = mybir.ActivationFunctionType
AXX = mybir.AxisListType.X
MAX_OVER_PARTITIONS = bass.bass_isa.ReduceOp.max

P = 128
B, SEQ, D = 2, 1024, 128
VOCAB = 125
H, DH = 8, 64
NT = SEQ // P
TILES = B * NT
SPH = NT
SPB = H * SPH
CPH = NT // 2
CPB = H * CPH
CW = 2 * P
HALF = SEQ // 2
GROUP = 16
ES = 64
F = 32
PAIRS = B * SEQ // (2 * GROUP)
GROUPS = 2 * PAIRS
PPT = PAIRS // TILES
NK = ES * F // P
QMAX = 127.0
ROUND = 12582912.0
NEG = -3.0e38
EPS = 1e-5
TIE = 1e-6 / (GROUP - 1)
T_LAG, PV_LAG = 3, 5


def layer_kernel(nc, tok, emb, conv, w_pairs, wv, wqkv_rows, u_qkv, wo_pairs, wo_twice, wo_rows, u_out,
                 sigma_qkv, sigma_out, temperature, b_out, controller, f1, f2, out):
    with ExitStack() as ctx:
        def sb(name, shape, dt=F32):
            return ctx.enter_context(nc.sbuf_tensor(name, shape, dt))

        def sem(name):
            return ctx.enter_context(nc.semaphore(name))

        ps = ctx.enter_context(nc.psum_tensor("ps", [P, 8, 512], F32))
        SCORES, TRANS, PV_BANK, WORK = 0, 4, 6, 7

        ident = sb("ident", [P, P])
        ident_b = sb("ident_b", [P, P], BF16)
        neg_diag = sb("neg_diag", [P, P], BF16)
        ones = sb("ones", [P, P])
        quad = sb("quad", [P, 4])
        vocab_id = sb("vocab_id", [P, 1])
        tie = sb("tie", [P, GROUP])
        powers = sb("powers", [P, 3 * NT])
        emb_sb = sb("emb_sb", [P, D])
        conv_sb = sb("conv_sb", [P, 2, D])
        quant = sb("quant", [P, 3 * D])
        table = sb("table", [P, 2, D])
        qs = sb("qs", [P, 8])
        wv_sb = sb("wv_sb", [P, H * DH])
        wo_sb = sb("wo_sb", [P, H // 2, D])
        wo_last = sb("wo_last", [P, 2, D])
        sig = sb("sig", [P, 3])
        norm_sb = sb("norm_sb", [P, 32])
        w_slot = sb("w_slot", [P, 2, P])
        b_sb = sb("b_sb", [P, D])
        h_sb = sb("h_sb", [P, TILES, D])
        x2 = sb("x2", [P, TILES, D])
        x2t = sb("x2t", [P, B * SEQ])
        xt = sb("xt", [P, SEQ])
        stats = sb("stats", [P, TILES, 6])
        mv = sb("mv", [P, TILES, 2])
        rstd = sb("rstd", [P, TILES])
        q_st = sb("q_st", [P, 2, SEQ], F32R)
        k_hi = sb("k_hi", [P, 2, SEQ], F32R)
        k_lo = sb("k_lo", [P, 2, SEQ], F32R)
        v_all = sb("v_all", [P, NT, H, P], F32R)
        v_slot = sb("v_slot", [P, 2, NT, P], F32R)
        probs = sb("probs", [P, 4, SEQ])
        neg_max = sb("neg_max", [P, 4])
        row_sum = sb("row_sum", [P, 4])
        inv_sum = sb("inv_sum", [P, 4])
        pt_hi = sb("pt_hi", [P, 2, NT, CW], F32R)
        pt_lo = sb("pt_lo", [P, 2, NT, CW], F32R)
        arena = sb("arena", [P, 8 * SEQ])
        ctrl_sb = sb("ctrl_sb", [P, ES])
        f1_sb = sb("f1_sb", [P, ES * F])
        f2_sb = sb("f2_sb", [P, NK, D])
        group_max = sb("group_max", [P, PAIRS])

        probs_flat = probs[:, :, :].rearrange("p a b -> p (a b)")
        one_hot = [probs_flat[:, 2 * SEQ * b:2 * SEQ * b + SEQ + 1] for b in range(B)]
        x2_flat = x2[:, :, :].rearrange("p t d -> p (t d)")
        tok_sb = [x2_flat[:, SEQ * b:SEQ * (b + 1)].bitcast(I32) for b in range(B)]
        hidden = probs_flat[:, 0:2 * SEQ].rearrange("p (r n) -> p r n", r=4)
        result = probs_flat[:, 2 * SEQ:4 * SEQ].rearrange("p (t d) -> p t d", d=D)
        perm = x2t[:, :].rearrange("p (j t) -> p j t", t=2 * GROUP)
        wu_sb = arena[:, 0:12 * P].rearrange("p (t d) -> p t d", d=D)
        wr_sb = arena[:, 12 * P:24 * P].rearrange("p (t d) -> p t d", d=D)
        wor_sb = arena[:, 24 * P:24 * P + H * DH]
        wou_sb = arena[:, 28 * P:28 * P + H * DH]
        uo_row, u_row = xt[:, 0:H * DH], xt[:, H * DH:H * DH + D]
        x_hat = [arena[:, 4 * SEQ:5 * SEQ].rearrange("p (t d) -> p t d", d=D), x2[:, NT:TILES, :]]
        pair_qk = arena[:, 0:4 * SEQ].rearrange("p (w l n) -> p w l n", w=2, l=2)
        o_slot = arena[:, 4 * SEQ:6 * SEQ].rearrange("p (s n) -> p s n", s=2)
        o_pair = arena[:, 6 * SEQ:8 * SEQ].rearrange("p (s n) -> p s n", s=2)
        inter_p = arena[:, :].rearrange("p (j d) -> p j d", d=D)
        v_flat = v_all[:, :, :, :].rearrange("p t h c -> p (t h c)").bitcast(F32)
        taken = v_flat.rearrange("p (e g) -> p e g", g=GROUPS)
        inter_t = v_flat.rearrange("p (j r) -> p j r", r=P)
        pt_lo_flat = pt_lo[:, :, :, :].rearrange("p a t c -> p (a t c)")
        spread = q_st[:, :, :].rearrange("p s (r j c) -> p (s r) j c", r=2, c=P)
        x2_hi = [a.rearrange("p (t d) -> p t d", d=D) for a in (k_hi[:, 0, :], pt_lo_flat[:, 0:SEQ])]
        x2_lo = [a.rearrange("p (t d) -> p t d", d=D)
                 for a in (k_lo[:, 0, :], pt_lo_flat[:, SEQ:2 * SEQ])]
        logits = arena[:, 0:SEQ]

        wait_passed = sem("wait_passed")
        const_ready = sem("const_ready")
        tok_loaded = [sem(f"tok_loaded{b}") for b in range(B)]
        tables_loaded = sem("tables_loaded")
        wqkv_loaded = sem("wqkv_loaded")
        wout_loaded = sem("wout_loaded")
        attn_loaded = sem("attn_loaded")
        ffn_loaded = sem("ffn_loaded")
        setup_dve = sem("setup_dve")
        setup_pe = sem("setup_pe")
        setup_act = sem("setup_act")
        setup_pool = sem("setup_pool")
        one_hot_ready = sem("one_hot_ready")
        h_mm = sem("h_mm")
        h_ready = sem("h_ready")
        stat_done = sem("stat_done")
        setup_norm = sem("setup_norm")
        aggr_done = sem("aggr_done")
        rstd_done = sem("rstd_done")
        xhat_done = sem("xhat_done")
        bias_added = sem("bias_added")
        xt_mm = sem("xt_mm")
        xt_done = sem("xt_done")
        v_mm = sem("v_mm")
        v_hi_done = sem("v_hi_done")
        v_lo_done = sem("v_lo_done")
        w_loaded = sem("w_loaded")
        qk_loaded = [sem(f"qk_loaded{i}") for i in range(2)]
        vs_loaded = [sem(f"vs_loaded{i}") for i in range(2)]
        work_mm = sem("work_mm")
        work_hi = sem("work_hi")
        work_read = sem("work_read")
        scores_ready = sem("scores_ready")
        max_done = sem("max_done")
        exp_done = sem("exp_done")
        recip_done = sem("recip_done")
        norm_done = sem("norm_done")
        pt_ready = sem("pt_ready")
        hi_done = sem("hi_done")
        lo_done = sem("lo_done")
        pv_done = sem("pv_done")
        o_done = sem("o_done")
        o_moved = [sem(f"o_moved{i}") for i in range(2)]
        o_summed = sem("o_summed")
        x2_done = sem("x2_done")
        x2t_mm = sem("x2t_mm")
        x2t_done = sem("x2t_done")
        perm_zero = sem("perm_zero")
        logit_mm = sem("logit_mm")
        choose = sem("choose")
        x2_hi_done = sem("x2_hi_done")
        x2_lo_done = sem("x2_lo_done")
        permt_mm = sem("permt_mm")
        spread_done = sem("spread_done")
        taken_mm = sem("taken_mm")
        taken_done = sem("taken_done")
        hid_mm = sem("hid_mm")
        hid_done = sem("hid_done")
        int_mm = sem("int_mm")
        int_done = sem("int_done")
        intp_mm = sem("intp_mm")
        intp_done = sem("intp_done")
        res_mm = sem("res_mm")
        result_done = sem("result_done")
        stored = sem("stored")

        N_CONST = 14

        def wait_apart(engine, semaphore, value):
            engine.wait_ge(semaphore, value)
            engine.sem_inc(wait_passed, 1)

        SUM = {(1, 2): "s0", (1, 4): "s1"}
        QK = {(0, 3): "q0", (0, 5): "q1", (0, 7): "k0", (1, 1): "k1"}
        MID = {**QK, **SUM}
        FIRST = {(0, 0): "e2", (0, 1): "e3", **QK}
        SWITCH = {(0, 0): "x0", (0, 1): "x1", (0, 2): "q0", (0, 3): "q1", (0, 5): "k0", (0, 7): "k1",
                  (1, 0): "v0", (1, 1): "v1", (1, 3): "v2", (1, 5): "v3", (1, 6): "v4", (1, 7): "v5", **SUM}
        AGAIN = {(0, 0): "v6", (0, 1): "v7", **MID}
        LAST = {**SUM, (1, 3): "t0", (1, 5): "t1", (1, 7): "l0"}
        PAIR_WORK = [FIRST, MID, MID, SWITCH, AGAIN, MID, MID, LAST, {}]

        def order(work):
            return sorted(work)

        def highs(work):
            return [x for x in order(work) if work[x][0] in "qkv"]

        USES = [4 + sum(len(w) for w in PAIR_WORK[:i]) for i in range(9)]
        HIGHS = [4 + sum(len(highs(w)) for w in PAIR_WORK[:i]) for i in range(9)]

        NORMS = [(0, 4), (4, 8), (8, 16), (0, 8), (8, 12), (12, 16)]
        TILES_BEFORE = [sum(b - a for a, b in NORMS[:g]) for g in range(len(NORMS))]

        LAST_OUTPUTS = [(0, 0, WORK), (0, 1, TRANS), (1, 0, TRANS + 1), (1, 1, WORK)]

        def transposes_bank(t, a, drain):
            return 2 * (t - 1) + a if drain and t > 0 else TRANS + a

        CHOICES = (0, 1, PV_BANK, WORK)
        TAKEN = 2
        SETUP_QK = {"k0": WORK, "k1": 0, "q0": 1, "q1": 2}

        class Pair:

            def __init__(self, i, p=0):
                self.work, self.i = PAIR_WORK[i], i
                self.index = p + i
                self.step0 = 2 * SPH * p + 2 * SPH * i
                self.chunk0 = 2 * CPH * p + 2 * CPH * i
                self.head_pair = p + i % 4
                self.head = 2 * p + 2 * (i % 4)
                self.uses = len(MID) * p + USES[i]
                self.highs = len(highs(MID)) * p + HIGHS[i]
                self.slot_loads = 16 * p + 16 * (i + 1)

            def use(self, k, t):
                return self.uses + order(self.work).index((k, t)) + 1

            def use_of(self, kind):
                return self.use(*next(x for x in self.work if self.work[x] == kind))

            def high(self, k, t):
                return self.highs + highs(self.work).index((k, t)) + 1

        def run_pairs(engine, pair_body):
            for first in (0, 4):
                pair_body(Pair(first))
                with engine.Fori(0, 2) as p:
                    pair_body(Pair(first + 1, p))
                pair_body(Pair(first + 3))

        block = ctx.enter_context(nc.Block())

        @block.gpsimd
        def _(pool):
            count = [0]

            def const(ins):
                ins.then_inc(const_ready, 1)
                count[0] += 1

            const(pool.memset(ones[:, :], 1.0))
            const(pool.memset(ident[:, :], 0.0))
            const(pool.memset(ident_b[:, :], 0.0))
            const(pool.memset(neg_diag[:, :], 0.0))
            const(pool.iota(vocab_id[:, :], [[0, 1]], base=0, channel_multiplier=1,
                            allow_small_or_imprecise_dtypes=True))
            const(pool.iota(tie[:, :], [[1, GROUP]], base=0, channel_multiplier=0,
                            allow_small_or_imprecise_dtypes=True))
            const(pool.memset(powers[:, 0:2 * NT], -0.5))
            const(pool.memset(powers[:, 2 * NT:3 * NT], 0.5))
            pool.wait_ge(const_ready, count[0])
            for m, fill in ((ident, 1.0), (ident_b, 1.0), (neg_diag, NEG)):
                const(pool.affine_select(out=m[:, :], in_=m[:, :], compare_op=ALU.not_equal, fill=fill,
                                         base=0, pattern=[[-1, P]], channel_multiplier=1))
            const(pool.affine_select(out=quad[:, :], in_=ones[:, 0:4], compare_op=ALU.is_ge, fill=0.0,
                                     base=0, pattern=[[-32, 4]], channel_multiplier=1))
            pool.wait_ge(const_ready, count[0])
            const(pool.affine_select(out=quad[:, :], in_=quad[:, :], compare_op=ALU.is_ge, fill=0.0,
                                     base=31, pattern=[[32, 4]], channel_multiplier=-1))
            const(pool.tensor_scalar(tie[:, :], tie[:, :], TIE, 1.0, ALU.mult, ALU.mult))
            assert count[0] == N_CONST
            pool.wait_ge(setup_dve, 3)
            pool.partition_all_reduce(qs[:, 1:2], qs[:, 0:1], P, MAX_OVER_PARTITIONS).then_inc(setup_pool, 1)
            pool.wait_ge(wqkv_loaded, 32)
            pool.tensor_tensor(wu_sb, wr_sb, u_row.unsqueeze(1).broadcast_to([P, 12, D]), ALU.mult
                               ).then_inc(setup_pool, 1)
            pool.wait_ge(wout_loaded, 16 * 5)
            pool.tensor_tensor(wou_sb, wor_sb, uo_row, ALU.mult).then_inc(setup_pool, 1)

            def deviations(g):
                tiles = slice(*NORMS[g])
                pool.wait_ge(aggr_done, g + 1)
                pool.tensor_tensor(rstd[:, tiles], rstd[:, tiles], powers[:, 0:tiles.stop - tiles.start], ALU.pow
                                   ).then_inc(rstd_done, 1)

            deviations(0)
            deviations(1)
            pool.wait_ge(setup_dve, SETUP_RATIO)
            pool.tensor_tensor(norm_sb[:, 26:28], norm_sb[:, 24:26], powers[:, 2 * NT:2 * NT + 2],
                               ALU.pow).then_inc(setup_pool, 1)

            def add_bias(b):
                pool.wait_ge(xhat_done, NT * (b + 1))
                pool.tensor_tensor(h_sb[:, b * NT:(b + 1) * NT, :], h_sb[:, b * NT:(b + 1) * NT, :],
                                   b_sb[:, :].unsqueeze(1).broadcast_to([P, NT, D]), ALU.add).then_inc(bias_added, 1)

            pool.wait_ge(attn_loaded, 64)
            add_bias(0)

            def quarter(parts, j):
                return parts[j // 2][:, 4 * (j % 2):4 * (j % 2) + 4, :]

            def token_high(j):
                pool.wait_ge(x2_done, 4 * j + 4)
                pool.tensor_copy(quarter(x2_hi, j), x2[:, 4 * j:4 * j + 4, :]).then_inc(x2_hi_done, 1)

            def token_low(j):
                pool.wait_ge(x2_hi_done, j + 1)
                pool.tensor_tensor(quarter(x2_lo, j), x2[:, 4 * j:4 * j + 4, :], quarter(x2_hi, j).bitcast(F32),
                                   ALU.subtract).then_inc(x2_lo_done, 1)

            def clear_choices(b):
                pool.memset(perm[:, b * PAIRS // 2:(b + 1) * PAIRS // 2, :], 0.0).then_inc(perm_zero, 1)

            def divide(pair):
                for k in range(2):
                    for t in range(SPH):
                        wait_apart(pool, recip_done, pair.step0 + k * SPH + t + 1)
                        pool.tensor_scalar(probs[:, t % 4, :], probs[:, t % 4, :], inv_sum[:, t % 4:t % 4 + 1],
                                           1.0, ALU.mult, ALU.mult).then_inc(norm_done, 1)
                        if (k, t) == (0, 6) and pair.i == 0:
                            deviations(2)
                        if (k, t) == (0, 6) and pair.i == 7:
                            deviations(3)
                        if k == 1 and t < 2 and pair.i > 0:
                            if t == 0:
                                for moved in o_moved:
                                    wait_apart(pool, moved, 32 * pair.index)
                            half = slice(t * HALF, (t + 1) * HALF)
                            pool.tensor_tensor(o_pair[:, 0, half], o_pair[:, 0, half], o_pair[:, 1, half],
                                               ALU.add).then_inc(o_summed, 1)
                        if (k, t) == (1, 4) and pair.i == 7:
                            pool.wait_ge(scores_ready, B * SPB - SPH)
                            token_high(0)
                        if (k, t) == (1, 5) and pair.i == 7:
                            token_high(1)
                        if (k, t) == (1, 7) and pair.i == 0:
                            add_bias(1)

            run_pairs(pool, divide)
            pool.wait_ge(work_mm, Pair(7).use_of("l0"))
            clear_choices(0)
            token_low(0)
            token_low(1)
            deviations(4)
            deviations(5)
            pool.wait_ge(logit_mm, 1)
            clear_choices(1)
            token_low(2)
            token_low(3)

        @block.sync
        def _(sp):
            sp.dma_start(emb_sb[0:VOCAB, :], emb).then_inc(tables_loaded, 16)
            sp.dma_start(conv_sb[0:VOCAB, :, :].rearrange("p k d -> p (k d)"),
                         conv.rearrange("(o k) d -> o (k d)", o=1).partition_broadcast(VOCAB)
                         ).then_inc(tables_loaded, 16)
            for b in range(B):
                sp.dma_start(tok_sb[b], tok[b:b + 1, :].partition_broadcast(P)).then_inc(tok_loaded[b], 16)

            def weights(index):
                sp.dma_start(w_slot[:, :, :].rearrange("p w c -> p (w c)"), w_pairs[index, :, :]
                             ).then_inc(w_loaded, 16)

            def head_part(k, which):
                rows = slice(DH * k, DH * (k + 1))
                for part in range(2):
                    half = slice(DH * part, DH * (part + 1))
                    for dst, w, low in ((q_st, 0, part), (k_hi, 1, 0), (k_lo, 1, 1)):
                        if w == which:
                            sp.dma_start(dst[half, k, :].bitcast(F32), pair_qk[rows, w, low, :]
                                         ).then_inc(qk_loaded[k], 16)

            def head_qk(k):
                head_part(k, 0)
                head_part(k, 1)

            def head_v(h, k):
                sp.dma_start(v_slot[:, k, :, :].bitcast(F32), v_all[:, :, h, :].bitcast(F32)
                             ).then_inc(vs_loaded[k], 16)

            sp.dma_start(uo_row, u_out.partition_broadcast(P)).then_inc(wout_loaded, 16)
            sp.dma_start(wor_sb, wo_rows).then_inc(wout_loaded, 16)
            weights(0)
            sp.dma_start(wv_sb[:, :], wv).then_inc(attn_loaded, 16)
            sp.dma_start(b_sb[:, :], b_out.partition_broadcast(P)).then_inc(attn_loaded, 16)
            sp.dma_start(wo_sb[:, :, :], wo_pairs).then_inc(attn_loaded, 16)
            sp.dma_start(wo_last[:, :, :], wo_twice).then_inc(attn_loaded, 16)
            sp.dma_start(ctrl_sb[:, :], controller).then_inc(ffn_loaded, 16)
            sp.dma_start(f1_sb[:, :], f1).then_inc(ffn_loaded, 16)
            sp.dma_start(f2_sb[:, :, :], f2).then_inc(ffn_loaded, 16)
            sp.wait_ge(work_read, 2)
            head_part(0, 1)
            sp.wait_ge(work_read, 4)
            head_part(0, 0)
            weights(1)
            sp.wait_ge(v_lo_done, NT)
            head_v(0, 0)

            def move_output(k):
                side = slice(DH * k, DH * (k + 1))
                for part in range(2):
                    sp.dma_start(o_pair[side, part, :], o_slot[DH * part:DH * (part + 1), k, :]
                                 ).then_inc(o_moved[k], 16)

            def pair_loads(pair):
                if pair.i > 0:
                    wait_apart(sp, scores_ready, pair.step0)
                head_qk(1)
                if pair.i == 4:
                    wait_apart(sp, work_read, pair.use_of("v7"))
                    wait_apart(sp, pv_done, pair.chunk0 - CPH)
                    head_v(0, 0)
                if pair.i > 0:
                    wait_apart(sp, pv_done, pair.chunk0)
                head_v(pair.head + 1, 1)
                if pair.i > 0:
                    wait_apart(sp, o_done, pair.chunk0)
                    move_output(1)
                if pair.i < 7:
                    wait_apart(sp, work_mm, pair.use_of("k1"))
                    weights(pair.head_pair + 2)
                    wait_apart(sp, work_read, pair.use_of("k1"))
                    wait_apart(sp, scores_ready, pair.step0 + SPH)
                    head_qk(0)
                    if pair.i != 3:
                        wait_apart(sp, pv_done, pair.chunk0 + CPH)
                        head_v(pair.head + 2, 0)
                    if pair.i > 0:
                        wait_apart(sp, work_mm, pair.use_of("s1"))
                    wait_apart(sp, o_done, pair.chunk0 + CPH)
                    move_output(0)

            run_pairs(sp, pair_loads)

            for t in range(TILES):
                sp.wait_ge(result_done, t + 1)
                sp.dma_start(out[t * P:(t + 1) * P, :], result[:, t, :]).then_inc(stored, 16)
            sp.wait_ge(stored, 16 * TILES)

        @block.tensor
        def _(pe):
            def embed(c):
                b, bank = c // 2, c if c < 2 else WORK
                for t in range(4 * (c % 2), 4 * (c % 2) + 4):
                    dst = ps[:, bank, (t % 4) * P:(t % 4 + 1) * P]
                    pe.matmul(dst, one_hot[b][:, t * P:(t + 1) * P], table[:, 0, :], start=True, stop=False)
                    ins = pe.matmul(dst, one_hot[b][:, 1 + t * P:1 + (t + 1) * P], table[:, 1, :],
                                    start=False, stop=True)
                return ins

            pe.wait_ge(setup_dve, SETUP_TABLES)
            pe.wait_ge(one_hot_ready, 2)
            embed(0).then_inc(h_mm, 1)
            embed(1).then_inc(h_mm, 1)
            pe.wait_ge(setup_dve, SETUP_VECTORS)
            for t in range(12):
                last = pe.matmul(ps[:, 6, 0:1], wr_sb[:, t, :], norm_sb[:, t:t + 1],
                                 start=t == 0, stop=t == 11)
            last.then_inc(setup_pe, 1)
            for t in range(4):
                last = pe.matmul(ps[:, 7, t:t + 1], wor_sb[:, t * P:(t + 1) * P], norm_sb[:, 12:13],
                                 start=True, stop=True)
            last.then_inc(setup_pe, 1)
            pe.wait_ge(setup_act, 3)
            pe.wait_ge(const_ready, N_CONST)
            for t in range(NT):
                pe.wait_ge(xhat_done, t + 1)
                ins = pe.transpose(ps[:, 5 + t // 4, (t % 4) * P:(t % 4 + 1) * P], x_hat[0][:, t, :], ident[:, :])
                if t % 4 == 3:
                    ins.then_inc(xt_mm, 1)

            def project_values(t, bank):
                return pe.matmul(ps[:, bank, :], xt[:, t * P:(t + 1) * P], wv_sb[:, :], start=True, stop=True)

            def project_qk(kind, bank=WORK):
                which, c = "qk".index(kind[0]), int(kind[1])
                return pe.matmul(ps[:, bank, :], w_slot[:, which, :], xt[:, c * HALF:(c + 1) * HALF],
                                 start=True, stop=True)

            pe.wait_ge(h_ready, 2)
            pe.wait_ge(w_loaded, 16)
            for kind in SETUP_QK:
                pe.wait_ge(xt_done, int(kind[1]) + 1)
                project_qk(kind, SETUP_QK[kind]).then_inc(work_mm, 1)
                if kind == "k0":
                    pe.wait_ge(setup_dve, SETUP_SQUARES)
                    pe.matmul(ps[:, 4, 0:4], ones[:, :], norm_sb[:, 18:22], start=True, stop=True
                              ).then_inc(setup_pe, 1)
            pe.wait_ge(attn_loaded, 64)
            pe.wait_ge(setup_dve, SETUP_RATIO)
            for t in range(NT):
                if t == 3:
                    pe.wait_ge(work_read, 1)
                if t >= 4:
                    pe.wait_ge(v_lo_done, t - 3)
                project_values(t, 4 + t % 4).then_inc(v_mm, 1)
            pe.wait_ge(work_read, 4)

            def scores(pair, k, t):
                n = pair.step0 + k * SPH + t
                if t == 0:
                    pe.wait_ge(qk_loaded[k], 6 * pair.slot_loads)
                if not (pair.i == 0 and k == 0 and t < 2):
                    pe.wait_ge(exp_done, n - 1)
                for c in range(2):
                    bank = ps[:, SCORES + 2 * (t % 2) + c, :]
                    q = q_st[:, k, t * P:(t + 1) * P]
                    half = slice(c * HALF, (c + 1) * HALF)
                    pe.matmul(bank, q, k_hi[:, k, half], start=True, stop=False)
                    if c == t // 4:
                        pe.matmul(bank[:, (t % 4) * P:(t % 4 + 1) * P], neg_diag[:, :], ident_b[:, :],
                                  start=False, stop=False)
                    ins = pe.matmul(bank, q, k_lo[:, k, half], start=False, stop=True)
                ins.then_inc(scores_ready, 1)

            def transposes(n, t, a, bank, begins):
                m = n - T_LAG
                if a == 0:
                    pe.wait_ge(norm_done, m + 1)
                if not begins:
                    pe.wait_ge(lo_done, 2 * m - 1 + a)
                for q in range(4):
                    col = (4 * a + q) * P
                    ins = pe.transpose(ps[:, bank, q * P:(q + 1) * P],
                                       probs[:, (t - T_LAG) % 4, col:col + P], ident[:, :])
                ins.then_inc(pt_ready, 1)

            def values(chunk, c_local, slot, slot_loads, quarter, begins):
                if quarter == 0:
                    pe.wait_ge(lo_done, 4 * chunk + 4)
                    if not begins:
                        pe.wait_ge(o_done, chunk)
                    if c_local == 0:
                        pe.wait_ge(vs_loaded[slot], slot_loads)
                for jt in (2 * quarter, 2 * quarter + 1):
                    for src in (pt_hi, pt_lo):
                        ins = pe.matmul(ps[:, PV_BANK, 0:CW], v_slot[:, slot, jt, :], src[:, c_local % 2, jt, :],
                                        start=jt == 0 and src is pt_hi, stop=jt == NT - 1 and src is pt_lo)
                if quarter == 3:
                    ins.then_inc(pv_done, 1)

            def lagging(pair, k, t, drain=False):
                n = pair.step0 + k * SPH + t
                fresh = pair.i == 0 and k == 0
                tr = not (fresh and t < T_LAG) and not (drain and t >= T_LAG)
                late = t - PV_LAG - (t % 2 == 0)
                pv = not (fresh and late < 0) and not (drain and late >= 0)
                c_local = late // 2 % CPH
                chunk = pair.chunk0 + k * CPH + late // 2
                slot = k if late >= 0 else 1 - k
                loads = pair.slot_loads - (16 if k == 0 and late < 0 else 0)
                if fresh and t == T_LAG:
                    pe.wait_ge(v_lo_done, NT)
                for half in range(2):
                    if tr:
                        transposes(n, t, half, transposes_bank(t, half, drain),
                                   (fresh and t == T_LAG) or (drain and t > 0))
                    if half == 1:
                        work(pair, k, t)
                    if pv:
                        values(chunk, c_local, slot, loads, half + (2 if t % 2 == 0 else 0),
                               fresh and t == PV_LAG)

            def expert_logits(b, bank):
                x2_pairs = x2t[:, :].rearrange("p (j u t) -> p j u t", u=2, t=GROUP)
                for u in range(2):
                    ins = pe.matmul(ps[u * ES:(u + 1) * ES, bank, :], ctrl_sb[:, :],
                                    x2_pairs[:, b * PAIRS // 2:(b + 1) * PAIRS // 2, u, :], start=True, stop=True)
                return ins

            def project_output(src, weights, c, bank):
                for j in range(4):
                    tile = 4 * c + j
                    ins = pe.matmul(ps[:, bank, j * P:(j + 1) * P], src[:, tile * P:(tile + 1) * P], weights,
                                    start=True, stop=True)
                return ins

            def work(pair, k, t):
                kind = pair.work.get((k, t))
                if not kind:
                    return
                pe.wait_ge(work_read, pair.use(k, t) - 1)
                if kind == "q0":
                    pe.wait_ge(w_loaded, 16 * (pair.index + 2))
                if kind in ("q0", "q1") and pair.i == 3:
                    pe.wait_ge(xt_done, 2 + int(kind[1]) + 1)
                if kind[0] in "qk":
                    ins = project_qk(kind)
                elif kind[0] == "v":
                    ins = project_values(int(kind[1]), WORK)
                elif kind[0] == "e":
                    pe.wait_ge(one_hot_ready, 2 * B)
                    pe.wait_ge(v_lo_done, NT)
                    ins = embed(int(kind[1]))
                elif kind[0] in "xt":
                    c = int(kind[1])
                    if kind[0] == "x":
                        pe.wait_ge(xhat_done, 2 * NT)
                    else:
                        pe.wait_ge(x2_done, 4 * c + 4)
                    for j in range(4 * c, 4 * c + 4):
                        src = x_hat[1][:, j, :] if kind[0] == "x" else x2[:, j, :]
                        ins = pe.transpose(ps[:, WORK, j % 4 * P:(j % 4 + 1) * P], src, ident[:, :])
                elif kind == "l0":
                    pe.wait_ge(ffn_loaded, 48)
                    pe.wait_ge(x2t_done, 2)
                    ins = expert_logits(0, WORK)
                else:
                    c = int(kind[1])
                    pe.wait_ge(o_summed, 2 * pair.index - 1 + c)
                    ins = project_output(o_pair[:, 0, :],
                                         wo_sb[:, (pair.head_pair - 1 if pair.i % 4 else H // 2 - 1), :], c, WORK)
                ins.then_inc(work_mm, 1)

            def pair_steps(pair):
                for k in range(2):
                    for t in range(SPH):
                        scores(pair, k, t)
                        lagging(pair, k, t)

            run_pairs(pe, pair_steps)

            def choice_transposes(b):
                pe.wait_ge(choose, 4 * (b + 1))
                for i in range(NT * b, NT * (b + 1)):
                    ins = pe.transpose(ps[:, CHOICES[i // 4], i % 4 * P:(i % 4 + 1) * P], x2t[:, i * P:(i + 1) * P],
                                       ident[:, :])
                    if i % 4 == 3:
                        ins.then_inc(permt_mm, 1)

            def take(tiles):
                for i in tiles:
                    if i % 4 == 0:
                        pe.wait_ge(x2_lo_done, i // 4 + 1)
                    pe.wait_ge(spread_done, i + 1)
                    if i >= 4:
                        pe.wait_ge(taken_done, i - 3)
                    mov = spread[:, i % 4, :, :]
                    b, t = i // NT, i % NT
                    pe.matmul(ps[:, TAKEN + i % 4, :], x2_hi[b][:, t, :], mov, start=True, stop=False)
                    pe.matmul(ps[:, TAKEN + i % 4, :], x2_lo[b][:, t, :], mov, start=False, stop=True
                              ).then_inc(taken_mm, 1)

            drain = Pair(8)

            def last_output(i):
                head, c, bank = LAST_OUTPUTS[i]
                pe.wait_ge(o_done, B * CPB - (1 - head) * CPH - (2 if c == 0 else 0))
                if i in (0, 3):
                    pe.wait_ge(work_read, drain.uses + (1 if i == 3 else 0))
                else:
                    pe.wait_ge(lo_done, 2 * (B * SPB - 2))
                project_output(o_slot[:, head, :], wo_last[:, head, :], c, bank).then_inc(work_mm, 1)

            for t in range(T_LAG):
                lagging(drain, 0, t, drain=True)
            for i in range(3):
                last_output(i)
            for t in range(T_LAG, PV_LAG):
                lagging(drain, 0, t, drain=True)
            last_output(3)
            choice_transposes(0)

            for t in range(NT):
                pe.wait_ge(x2_done, NT + t + 1)
                ins = pe.transpose(ps[:, TRANS + t // 4, (t % 4) * P:(t % 4 + 1) * P], x2[:, NT + t, :], ident[:, :])
                if t % 4 == 3:
                    ins.then_inc(x2t_mm, 1)
            take(range(0, 1))
            pe.wait_ge(x2t_done, 4)
            expert_logits(1, PV_BANK).then_inc(logit_mm, 1)
            take(range(1, 5))
            choice_transposes(1)
            take(range(5, TILES))
            pe.wait_ge(taken_done, TILES)
            for k in range(NK):
                for q in range(4):
                    e = 4 * k + q
                    ins = pe.matmul(ps[32 * q:32 * (q + 1), k // 4, (k % 4) * GROUPS:(k % 4 + 1) * GROUPS],
                                    f1_sb[:, e * F:(e + 1) * F], taken[:, e, :], start=True, stop=True,
                                    tile_position=(0, 32 * q))
                if k % 4 == 3:
                    ins.then_inc(hid_mm, 1)
            for k in range(NK):
                pe.wait_ge(hid_done, k + 1)
                if k >= 2:
                    pe.wait_ge(int_done, k - 1)
                pe.matmul(ps[:, 4 + k % 2, :], f2_sb[:, k, :], hidden[:, k % 4, :],
                          start=True, stop=True).then_inc(int_mm, 1)
            pe.wait_ge(int_done, NK)

            def pair_transposes(i):
                if i >= 2:
                    pe.wait_ge(intp_done, i - 1)
                for j in range(PPT):
                    ins = pe.transpose(ps[:, 6 + i % 2, j * P:(j + 1) * P], inter_t[:, PPT * i + j, :], ident[:, :])
                ins.then_inc(intp_mm, 1)

            pair_transposes(0)
            for i in range(TILES):
                if i + 1 < TILES:
                    pair_transposes(i + 1)
                pe.wait_ge(intp_done, i + 1)
                if i >= 4:
                    pe.wait_ge(result_done, i - 3)
                for j in range(PPT):
                    ins = pe.matmul(ps[32 * j:32 * (j + 1), i % 4, 0:D], perm[:, PPT * i + j, :],
                                    inter_p[:, PPT * i + j, :], start=True, stop=True, tile_position=(0, 32 * j))
                ins.then_inc(res_mm, 1)

        @block.scalar
        def _(act):
            act.dma_start(u_row, u_qkv.partition_broadcast(P)).then_inc(wqkv_loaded, 16)
            act.dma_start(wr_sb, wqkv_rows).then_inc(wqkv_loaded, 16)
            for i, x in enumerate((sigma_qkv, sigma_out, temperature)):
                act.dma_start(sig[:, i:i + 1], x.partition_broadcast(P)).then_inc(wout_loaded, 16)

            def embedded(c):
                act.wait_ge(h_mm, c + 1)
                act.activation(h_sb[:, 4 * c:4 * c + 4, :], ps[:, c, :].rearrange("p (t d) -> p t d", d=D),
                               ACT.Relu).then_inc(h_ready, 1)

            act.wait_ge(wout_loaded, 16 * 5)
            act.activation(norm_sb[:, 28:29], sig[:, 2:3], ACT.Exp).then_inc(setup_act, 1)
            embedded(0)
            embedded(1)
            act.wait_ge(setup_pe, 1)
            act.activation(norm_sb[:, 13:14], ps[:, 6, 0:1], ACT.Copy).then_inc(setup_act, 1)
            act.wait_ge(setup_pe, 2)
            act.activation(norm_sb[:, 14:18], ps[:, 7, 0:4], ACT.Copy).then_inc(setup_act, 1)
            for c in range(2):
                act.wait_ge(xt_mm, c + 1)
                act.activation(xt[:, c * HALF:(c + 1) * HALF], ps[:, 5 + c, :], ACT.Copy).then_inc(xt_done, 1)

            q_scale, v_scale = norm_sb[:, 31:32], norm_sb[:, 29:30]

            def high_qk(kind, bank=WORK):
                which, c = "qk".index(kind[0]), int(kind[1])
                dst = pair_qk[:, which, 0, c * HALF:(c + 1) * HALF].bitcast(F32R)
                if which == 0:
                    return act.activation(dst, ps[:, bank, :], ACT.Copy, scale=q_scale)
                return act.activation(dst, ps[:, bank, :], ACT.Copy)

            def high_values(t, bank):
                return act.activation(v_all[:, t, :, 0:DH], ps[:, bank, :].rearrange("p (h c) -> p h c", c=DH),
                                      ACT.Copy, scale=v_scale)

            for j, kind in enumerate(SETUP_QK):
                act.wait_ge(work_mm, j + 1)
                if kind == "q0":
                    act.wait_ge(setup_dve, SETUP_SCALES)
                high_qk(kind, SETUP_QK[kind]).then_inc(work_hi, 1)
            for t in range(NT):
                act.wait_ge(v_mm, t + 1)
                high_values(t, 4 + t % 4).then_inc(v_hi_done, 1)

            def work(pair, k, t):
                kind = pair.work.get((k, t))
                if not kind or kind[0] in "sl":
                    return
                act.wait_ge(work_mm, pair.use(k, t))
                if kind[0] in "qk":
                    if kind == "q0":
                        act.wait_ge(qk_loaded[1], 6 * pair.slot_loads)
                    high_qk(kind).then_inc(work_hi, 1)
                elif kind[0] == "v":
                    if kind == "v0":
                        act.wait_ge(vs_loaded[1], pair.slot_loads)
                    high_values(int(kind[1]), WORK).then_inc(work_hi, 1)
                elif kind[0] == "e":
                    tiles = slice(4 * int(kind[1]), 4 * int(kind[1]) + 4)
                    act.activation(h_sb[:, tiles, :], ps[:, WORK, :].rearrange("p (t d) -> p t d", d=D),
                                   ACT.Relu).then_inc(h_ready, 1)
                    act.wait_ge(h_ready, int(kind[1]) + 1)
                    act.sem_inc(work_read, 1)
                else:
                    c = int(kind[1])
                    dst, done, before = (xt, xt_done, 2) if kind[0] == "x" else (x2t, x2t_done, 0)
                    act.activation(dst[:, c * HALF:(c + 1) * HALF], ps[:, WORK, :], ACT.Copy).then_inc(done, 1)
                    act.wait_ge(done, before + c + 1)
                    act.sem_inc(work_read, 1)

            def lagging(pair, k, t, drain=False):
                n = pair.step0 + k * SPH + t
                fresh = pair.i == 0 and k == 0
                idle = (fresh and t < T_LAG) or (drain and t >= T_LAG)
                m_local = (t - T_LAG) % SPH
                for a in range(2):
                    if idle:
                        break
                    act.wait_ge(pt_ready, 2 * (n - T_LAG) + a + 1)
                    if a == 0 and not (fresh and t - T_LAG < 4):
                        act.wait_ge(pv_done, pair.chunk0 + k * CPH + (t - T_LAG) // 2 - 1)
                    dst = pt_hi[:, m_local // 2 % 2, 4 * a:4 * a + 4, (m_local % 2) * P:(m_local % 2 + 1) * P]
                    act.activation(dst, ps[:, transposes_bank(t, a, drain), :].rearrange("p (j c) -> p j c", c=P),
                                   ACT.Copy).then_inc(hi_done, 1)

            def output(pair, k, t, drain=False):
                c_local = (t - PV_LAG - 1) // 2
                if t % 2 or (pair.i == 0 and k == 0 and c_local < 0) or (drain and c_local >= 0):
                    return
                slot = k if c_local >= 0 else 1 - k
                cols = slice((c_local % CPH) * CW, (c_local % CPH + 1) * CW)
                act.wait_ge(pv_done, pair.chunk0 + k * CPH + c_local + 1)
                if c_local % CPH == 0 and pair.i > 0:
                    act.wait_ge(o_moved[slot], 32 * pair.index)
                act.activation(o_slot[:, slot, cols], ps[:, PV_BANK, 0:CW], ACT.Copy).then_inc(o_done, 1)

            def exponentials(pair, k, t):
                n = pair.step0 + k * SPH + t
                act.wait_ge(max_done, n + 1)
                if not (pair.i == 0 and k == 0 and t < 4):
                    act.wait_ge(pt_ready, 2 * n - 6)
                act.activation(probs[:, t % 4, :].rearrange("p (a c) -> p a c", a=2),
                               ps[:, SCORES + 2 * (t % 2):SCORES + 2 * (t % 2) + 2, :], ACT.Exp,
                               bias=neg_max[:, t % 4:t % 4 + 1],
                               accum_out=row_sum[:, t % 4:t % 4 + 1]).then_inc(exp_done, 1)

            def pair_steps(pair):
                for k in range(2):
                    for t in range(SPH):
                        lagging(pair, k, t)
                        work(pair, k, t)
                        output(pair, k, t)
                        exponentials(pair, k, t)

            run_pairs(act, pair_steps)

            def take(tiles):
                for i in tiles:
                    act.wait_ge(taken_mm, i + 1)
                    act.activation(taken[:, :, 8 * i:8 * i + 8].rearrange("p e g -> p g e"),
                                   ps[:, TAKEN + i % 4, :].rearrange("p (g e) -> p g e", e=ES),
                                   ACT.Copy).then_inc(taken_done, 1)

            for t in range(PV_LAG):
                lagging(Pair(8), 0, t, drain=True)
                output(Pair(8), 0, t, drain=True)
            act.wait_ge(vs_loaded[1], 16 * 8)
            for c in range(2):
                act.wait_ge(x2t_mm, c + 1)
                act.activation(x2t[:, (2 + c) * HALF:(3 + c) * HALF], ps[:, TRANS + c, :], ACT.Copy
                               ).then_inc(x2t_done, 1)
            take(range(0, 1))
            for c in range(2):
                act.wait_ge(x2_done, 4 * c + 12)
                act.activation(x2_hi[1][:, 4 * c:4 * c + 4, :], x2[:, NT + 4 * c:NT + 4 * c + 4, :], ACT.Copy
                               ).then_inc(x2_hi_done, 1)
            take(range(1, TILES))
            act.wait_ge(hid_mm, 4)
            inter_v = inter_t.rearrange("p j (u e) -> p e j u", u=2)
            for k in range(NK):
                act.wait_ge(int_mm, k + 1)
                act.activation(inter_v[:, 4 * k:4 * k + 4, :, :],
                               ps[:, 4 + k % 2, :].rearrange("p (q j u) -> p q j u", q=4, u=2),
                               ACT.Copy).then_inc(int_done, 1)
            for i in range(TILES):
                act.wait_ge(intp_mm, i + 1)
                act.activation(inter_p[:, PPT * i:PPT * (i + 1), :],
                               ps[:, 6 + i % 2, :].rearrange("p (j d) -> p j d", d=D), ACT.Copy).then_inc(intp_done, 1)

        @block.vector
        def _(dve):
            count = [0]

            def link(ins):
                count[0] += 1
                ins.then_inc(setup_dve, 1)
                dve.wait_ge(setup_dve, count[0])

            link(dve.memset(qs[:, :], 0.0))
            link(dve.memset(table[:, :, :], 0.0))
            dve.wait_ge(tables_loaded, 32)
            link(dve.tensor_reduce(qs[0:VOCAB, 0:1], emb_sb[0:VOCAB, :], AXX, ALU.max, apply_absolute_value=True))
            link(dve.tensor_reduce(qs[0:VOCAB, 2:3], conv_sb[0:VOCAB, :, :].rearrange("p k d -> p (k d)"), AXX,
                                   ALU.max, apply_absolute_value=True))
            dve.wait_ge(setup_pool, 1)
            link(dve.tensor_scalar(qs[0:VOCAB, 3:5], qs[0:VOCAB, 1:3], 1.0 / QMAX, None, ALU.mult))
            link(dve.reciprocal(qs[0:VOCAB, 5:7], qs[0:VOCAB, 3:5]))
            parts = [(emb_sb[0:VOCAB, :], quant[0:VOCAB, 0:D], 0),
                     (conv_sb[0:VOCAB, :, :].rearrange("p k d -> p (k d)"), quant[0:VOCAB, D:3 * D], 1)]
            for w, q, i in parts:
                link(dve.tensor_scalar(q, w, qs[0:VOCAB, 5 + i:6 + i], ROUND, ALU.mult, ALU.add))
                link(dve.tensor_scalar(q, q, ROUND, qs[0:VOCAB, 3 + i:4 + i], ALU.subtract, ALU.mult))
                link(dve.tensor_tensor(q, q, w, ALU.subtract))
                link(dve.tensor_tensor(q, w, q, ALU.add))
            for k in range(2):
                link(dve.tensor_tensor(table[0:VOCAB, k, :], quant[0:VOCAB, 0:D],
                                       quant[0:VOCAB, D * (k + 1):D * (k + 2)], ALU.mult))
            assert count[0] == SETUP_TABLES
            def rows_of(b):
                dve.wait_ge(tok_loaded[b], 16)
                dve.wait_ge(const_ready, N_CONST)
                dve.memset(one_hot[b][:, 0:1], 0.0).then_inc(one_hot_ready, 1)
                dve.tensor_scalar(one_hot[b][:, 1:SEQ + 1], tok_sb[b], float(VOCAB - 1), vocab_id[:, :],
                                  ALU.min, ALU.is_equal).then_inc(one_hot_ready, 1)

            rows_of(0)
            dve.wait_ge(setup_pool, 2)
            link(dve.tensor_reduce(norm_sb[:, 0:12], wu_sb, AXX, ALU.add))
            dve.wait_ge(setup_pool, 3)
            link(dve.tensor_reduce(norm_sb[:, 12:13], wou_sb, AXX, ALU.add))
            assert count[0] == SETUP_VECTORS
            rows_of(1)

            def tile_statistics(t):
                dve.bn_stats(stats[:, t, :], h_sb[:, t, :]).then_inc(stat_done, 1)

            def variances(g):
                first, end = NORMS[g]
                for t in range(first, end):
                    dve.wait_ge(stat_done, TILES_BEFORE[g] + t - first + 1)
                    ins = dve.bn_aggr(mv[:, t, :], stats[:, t, :])
                ins.then_inc(setup_norm, 1)
                dve.wait_ge(setup_norm, g + 1)
                dve.tensor_scalar(rstd[:, first:end], mv[:, first:end, 1], EPS, None, ALU.add).then_inc(aggr_done, 1)

            def normalise_tile(t, dst, done):
                dve.tensor_scalar(dst, h_sb[:, t, :], mv[:, t, 0:1], rstd[:, t:t + 1],
                                  ALU.subtract, ALU.mult).then_inc(done, 1)

            for g in range(2):
                dve.wait_ge(h_ready, g + 1)
                for t in range(*NORMS[g]):
                    tile_statistics(t)
                variances(g)
            for g in range(2):
                dve.wait_ge(rstd_done, g + 1)
                for t in range(*NORMS[g]):
                    normalise_tile(t, x_hat[0][:, t, :], xhat_done)
            dve.wait_ge(setup_act, 3)
            sq = norm_sb[:, 22:24]
            scratch = quant[:, 0:12]
            for a, n, col in ((0, 12, 18), (12, 1, 19), (13, 1, 20), (14, 4, 21)):
                v = norm_sb[:, a:a + n]
                link(dve.tensor_tensor(scratch[:, 0:n], v, v, ALU.mult))
                link(dve.tensor_reduce(norm_sb[:, col:col + 1], scratch[:, 0:n], AXX, ALU.add))
            assert count[0] == SETUP_SQUARES
            dve.wait_ge(setup_pe, 3)
            link(dve.reciprocal(sq, ps[:, 4, 2:4]))
            link(dve.tensor_tensor(norm_sb[:, 24:26], ps[:, 4, 0:2], sq, ALU.mult))
            assert count[0] == SETUP_RATIO
            dve.wait_ge(setup_pool, 4)
            dve.wait_ge(wout_loaded, 16 * 5)
            dve.wait_ge(setup_act, 3)
            link(dve.tensor_tensor(norm_sb[:, 29:31], norm_sb[:, 26:28], sig[:, 0:2], ALU.mult))
            link(dve.scalar_tensor_tensor(norm_sb[:, 31:32], norm_sb[:, 29:30], norm_sb[:, 28:29],
                                          norm_sb[:, 29:30], ALU.mult, ALU.mult))
            assert count[0] == SETUP_SCALES
            q_scale, v_scale, o_scale = norm_sb[:, 31:32], norm_sb[:, 29:30], norm_sb[:, 30:31]
            dve.wait_ge(const_ready, N_CONST)

            def low_qk(kind, bank=WORK):
                which, c = "qk".index(kind[0]), int(kind[1])
                high = pair_qk[:, which, 0, c * HALF:(c + 1) * HALF]
                dst = pair_qk[:, which, 1, c * HALF:(c + 1) * HALF].bitcast(F32R)
                if which == 0:
                    return dve.scalar_tensor_tensor(dst, ps[:, bank, :], q_scale, high, ALU.mult, ALU.subtract)
                return dve.tensor_tensor(dst, ps[:, bank, :], high, ALU.subtract)

            def low_values(t, bank):
                return dve.scalar_tensor_tensor(
                    v_all[:, t, :, DH:P], ps[:, bank, :].rearrange("p (h c) -> p h c", c=DH), v_scale,
                    v_all[:, t, :, 0:DH].bitcast(F32), ALU.mult, ALU.subtract)

            for j, kind in enumerate(SETUP_QK):
                dve.wait_ge(work_hi, j + 1)
                low_qk(kind, SETUP_QK[kind]).then_inc(work_read, 1)
            for t in range(NT):
                dve.wait_ge(v_hi_done, t + 1)
                low_values(t, 4 + t % 4).then_inc(v_lo_done, 1)

            def of_batch(a, b):
                return a[:, b * PAIRS // 2:(b + 1) * PAIRS // 2]

            logit = logits.rearrange("p (j t) -> p j t", t=GROUP)

            def break_ties(b, bank):
                return dve.tensor_tensor(of_batch(logit, b), ps[:, bank, :].rearrange("p (j t) -> p j t", t=GROUP),
                                         tie[:, :].unsqueeze(1).broadcast_to([P, PAIRS // 2, GROUP]), ALU.add)

            def largest(b):
                dve.tensor_reduce(of_batch(group_max, b), of_batch(logit, b), AXX, ALU.max).then_inc(choose, 1)

            def choices(b):
                dve.wait_ge(choose, 4 * b + 2)
                dve.wait_ge(perm_zero, b + 1)
                for u in range(2):
                    rows = slice(u * ES, (u + 1) * ES)
                    dve.tensor_tensor(of_batch(perm[rows, :, u * GROUP:(u + 1) * GROUP], b),
                                      of_batch(logit[rows, :, :], b),
                                      of_batch(group_max[rows, :], b).unsqueeze(2).broadcast_to(
                                          [ES, PAIRS // 2, GROUP]), ALU.is_equal).then_inc(choose, 1)

            def spread_choices(tiles):
                for i in tiles:
                    dve.wait_ge(permt_mm, i // 4 + 1)
                    if i >= 4:
                        dve.wait_ge(taken_mm, i - 3)
                    dve.tensor_tensor(spread[:, i % 4, :, :],
                                      ps[:, CHOICES[i // 4], i % 4 * P:(i % 4 + 1) * P].unsqueeze(1).broadcast_to([P, 4, P]),
                                      quad[:, :].unsqueeze(2).broadcast_to([P, 4, P]), ALU.mult
                                      ).then_inc(spread_done, 1)

            def spread_norm(b, first, k, t):
                if k == 0 and 2 <= t < 6:
                    if t == 2 and first:
                        dve.wait_ge(h_ready, 4)
                    for i in (2 * (t - 2), 2 * (t - 2) + 1):
                        tile_statistics(b * NT + i)
                elif k == 0 and t == 6:
                    variances(2 if first else 3)
                elif k == 1 and 1 <= t < 5:
                    if t == 1:
                        dve.wait_ge(rstd_done, 3 if first else 4)
                    for i in (2 * (t - 1), 2 * (t - 1) + 1):
                        if first:
                            normalise_tile(b * NT + i, x_hat[1][:, i, :], xhat_done)
                        else:
                            normalise_tile(b * NT + i, x2[:, b * NT + i, :], x2_done)

            def add_output(first, bank):
                tiles = slice(first, first + 4)
                dve.scalar_tensor_tensor(h_sb[:, tiles, :], ps[:, bank, :].rearrange("p (t d) -> p t d", d=D),
                                         o_scale, h_sb[:, tiles, :], ALU.mult, ALU.add).then_inc(work_read, 1)

            def work(pair, k, t):
                kind = pair.work.get((k, t))
                if not kind or kind[0] in "ext":
                    return
                if kind[0] == "s":
                    dve.wait_ge(work_mm, pair.use(k, t))
                    add_output((pair.i - 1) // 4 * NT + 4 * int(kind[1]), WORK)
                    return
                if kind == "l0":
                    dve.wait_ge(qk_loaded[1], 6 * 16 * 8)
                    dve.wait_ge(work_mm, pair.use(k, t))
                    break_ties(0, WORK).then_inc(work_read, 1)
                    return
                dve.wait_ge(work_hi, pair.high(k, t))
                if kind[0] == "v":
                    low_values(int(kind[1]), WORK).then_inc(work_read, 1)
                else:
                    low_qk(kind).then_inc(work_read, 1)

            def lagging(pair, k, t, drain=False):
                n = pair.step0 + k * SPH + t
                fresh = pair.i == 0 and k == 0
                if (fresh and t < T_LAG) or (drain and t >= T_LAG):
                    return
                m_local = (t - T_LAG) % SPH
                for a in range(2):
                    at = (slice(None), m_local // 2 % 2, slice(4 * a, 4 * a + 4),
                          slice((m_local % 2) * P, (m_local % 2 + 1) * P))
                    dve.wait_ge(hi_done, 2 * (n - T_LAG) + a + 1)
                    bank = transposes_bank(t, a, drain)
                    dve.tensor_tensor(pt_lo[at], ps[:, bank, :].rearrange("p (j c) -> p j c", c=P),
                                      pt_hi[at].bitcast(F32), ALU.subtract).then_inc(lo_done, 1)

            def reciprocals(pair, k, t):
                n = pair.step0 + k * SPH + t
                dve.wait_ge(exp_done, n)
                dve.reciprocal(inv_sum[:, (t - 1) % 4:(t - 1) % 4 + 1],
                               row_sum[:, (t - 1) % 4:(t - 1) % 4 + 1]).then_inc(recip_done, 1)

            def maxima(pair, k, t):
                n = pair.step0 + k * SPH + t
                dve.wait_ge(scores_ready, n + 1)
                dve.tensor_reduce(neg_max[:, t % 4:t % 4 + 1],
                                  ps[:, SCORES + 2 * (t % 2):SCORES + 2 * (t % 2) + 2, :].rearrange(
                                      "p a c -> p (a c)"), AXX, ALU.max, negate=True).then_inc(max_done, 1)

            def pair_steps(pair):
                for k in range(2):
                    for t in range(SPH):
                        maxima(pair, k, t)
                        if not (pair.i == 0 and k == 0 and t == 0):
                            reciprocals(pair, k, t)
                        lagging(pair, k, t)
                        work(pair, k, t)
                        if (k, t) == (1, 7) and pair.i in (0, 4):
                            dve.wait_ge(bias_added, 1 + pair.i // 4)
                        if pair.i == 0:
                            spread_norm(1, True, k, t)
                        elif pair.i == 7:
                            if k == 0 and t == 0:
                                dve.wait_ge(work_read, pair.uses)
                            spread_norm(0, False, k, t)

            run_pairs(dve, pair_steps)
            drain = Pair(8)
            reciprocals(drain, 0, 0)
            for t in range(T_LAG):
                lagging(drain, 0, t, drain=True)
                if t == 0:
                    dve.wait_ge(work_read, drain.uses)
                    dve.sem_inc(choose, 1)
                    largest(0)
            for i, (head, c, bank) in enumerate(LAST_OUTPUTS):
                if i > 1:
                    dve.wait_ge(work_read, drain.uses + i - 1)
                dve.wait_ge(work_mm, drain.uses + i + 1)
                add_output(NT + 4 * c, bank)
                if head == 1:
                    dve.wait_ge(work_read, drain.uses + i + 1)
                    for t in range(*NORMS[4 + c]):
                        tile_statistics(t)
                    variances(4 + c)
                if i == 2:
                    choices(0)
            for g in (4, 5):
                dve.wait_ge(rstd_done, g + 1)
                for t in range(*NORMS[g]):
                    normalise_tile(t, x2[:, t, :], x2_done)
            spread_choices(range(0, 5))
            dve.wait_ge(logit_mm, 1)
            break_ties(1, PV_BANK).then_inc(choose, 1)
            dve.wait_ge(choose, 5)
            largest(1)
            choices(1)
            spread_choices(range(5, TILES))
            for k in range(NK):
                dve.wait_ge(hid_mm, k // 4 + 1)
                if k >= 4:
                    dve.wait_ge(int_mm, k - 3)
                dve.scalar_tensor_tensor(
                    hidden[:, k % 4, :].rearrange("p (q g) -> p q g", q=4),
                    ps[:, k // 4, (k % 4) * GROUPS:(k % 4 + 1) * GROUPS].unsqueeze(1).broadcast_to([P, 4, GROUPS]),
                    0.0, quad[:, :].unsqueeze(2).broadcast_to([P, 4, GROUPS]), ALU.max,
                    ALU.mult).then_inc(hid_done, 1)
            for i in range(TILES):
                dve.wait_ge(res_mm, i + 1)
                dve.tensor_tensor(result[:, i, :], ps[:, i % 4, 0:D], h_sb[:, i, :], ALU.add).then_inc(result_done, 1)


SETUP_TABLES = 16
SETUP_VECTORS = SETUP_TABLES + 2
SETUP_SQUARES = SETUP_VECTORS + 8
SETUP_RATIO = SETUP_SQUARES + 2
SETUP_SCALES = SETUP_RATIO + 2


def kernel(**inputs):
    import concourse.bacc as bacc
    from concourse.bass_utils import run_bass_kernel_spmd

    a = {k: np.asarray(v) for k, v in inputs.items()}
    w = a["L0_attn_w_qkv"]
    wo = a["L0_attn_w_out"]

    pairs = w[:2 * H * DH].reshape(2, H // 2, P, D).transpose(1, 3, 0, 2).reshape(H // 2, D, 2 * P)
    wo_t = wo.reshape(D, H, DH).transpose(2, 1, 0)
    arrays = {
        "tok": a["x"].astype(np.int32, copy=False),
        "emb": a["L0_tok_emb_weight"],
        "conv": a["L0_tok_conv_weight"].reshape(D, 2).T,
        "w_pairs": np.concatenate([pairs, pairs[:2]], axis=0),
        "wv": w[2 * H * DH:].T,
        "wqkv_rows": w.reshape(12, P, D).transpose(1, 0, 2),
        "u_qkv": a["L0_attn_u_qkv"].reshape(1, D),
        "wo_pairs": wo_t.reshape(DH, H // 2, 2, D).transpose(2, 0, 1, 3).reshape(P, H // 2, D),
        "wo_twice": np.concatenate([wo_t[:, H - 2:], wo_t[:, H - 2:]], axis=0),
        "wo_rows": wo,
        "u_out": a["L0_attn_u_out"].reshape(1, H * DH),
        "sigma_qkv": a["L0_attn_sigma_qkv"].reshape(1, 1),
        "sigma_out": a["L0_attn_sigma_out"].reshape(1, 1),
        "temperature": a["L0_attn_temperature"].reshape(1, 1),
        "b_out": a["L0_attn_b_out"].reshape(1, D),
        "controller": a["L0_ffn_controller"].reshape(D, ES),
        "f1": a["L0_ffn_f1"].reshape(D, ES * F),
        "f2": a["L0_ffn_f2"].reshape(NK, P, D).transpose(1, 0, 2),
    }
    nc = bacc.Bacc("TRN2", target_bir_lowering=False, num_devices=1)
    feeds, args = {}, []
    for name, x in arrays.items():
        x = np.ascontiguousarray(x)
        feeds["in_" + name] = x
        args.append(nc.dram_tensor("in_" + name, x.shape, mybir.dt.from_np(x.dtype), kind="ExternalInput").ap())
    args.append(nc.dram_tensor("out_h", (B * SEQ, D), F32, kind="ExternalOutput").ap())
    layer_kernel(nc, *args)
    r = run_bass_kernel_spmd(nc, [feeds], core_ids=[0])
    return r.results[0]["out_h"].reshape(B, SEQ, D)
```
